# Optimizing a Trainium2 kernel written in Bass

```python
import numpy as np
import jax
import jax.numpy as jnp

def _softmax(x, axis=-1):
    return jax.nn.softmax(x, axis=axis)
def _gelu(x):
    return jax.nn.gelu(x, approximate=True)
def _silu(x):
    return jax.nn.silu(x)
def _sigmoid(x):
    return jax.nn.sigmoid(x)
def _layernorm(x, axis=-1, eps=1e-5):
    m = jnp.mean(x, axis=axis, keepdims=True)
    v = jnp.var(x, axis=axis, keepdims=True)
    return (x - m) / jnp.sqrt(v + eps)
def _scatter_add(tgt, idx, src, axis=0):
    return tgt.at[idx].add(src)
def _segment_sum(src, seg, n):
    return jax.ops.segment_sum(src, seg, n)

kernel_name = 'mk_adj_preln_d2_adj_128_f04f2d'

def setup_inputs(seed: int = 0):
    np.random.seed(seed)
    _w = jnp.asarray
    def _rec_inputs():
        import jax
        import jax.numpy as jnp
        _gk = jax.random.key(seed)
        x = -0.000929 + 1 * jax.random.normal(jax.random.fold_in(_gk, 1), (8192, 128), jnp.float32)
        _w = (1.0 + jnp.arange(8192, dtype=jnp.float32)) ** -0.5
        _w = _w / _w.mean()
        _pij = jnp.clip(0.000976562 * _w[:, None] * _w[None, :], 0.0, 1.0)
        _a = jax.random.uniform(jax.random.fold_in(_gk, 2), (8192, 8192)) < _pij
        _a = jnp.logical_or(_a, jnp.eye(8192, dtype=bool))
        _af = _a.astype(jnp.float32)
        adj = _af
        return x, adj
    x, adj = _rec_inputs()
    def _L0_gnn_setup():
        import jax, jax.numpy as jnp
        import numpy as np
        N, DIN, DOUT = (8192, 128, 128)
        NEG = -9000000000000000.0
        ALPHA = 0.2
        key = jax.random.key(seed)
        kx, ka, kw, ks, kr = jax.random.split(key, 5)
        X = jax.random.normal(kx, (N, DIN), dtype=jnp.float32)
        A = (jax.random.uniform(ka, (N, N)) < 0.01).astype(jnp.float32)
        A = A.at[jnp.arange(N), jnp.arange(N)].set(1.0)
        lim_w = float(np.sqrt(6.0 / (DIN + DOUT)))
        W = jax.random.uniform(kw, (DOUT, DIN), jnp.float32, -lim_w, lim_w)
        b = jnp.zeros((DOUT,), jnp.float32)
        lim_a = float(np.sqrt(6.0 / (DOUT + 1)))
        a_s = jax.random.uniform(ks, (DOUT, 1), jnp.float32, -lim_a, lim_a)
        a_r = jax.random.uniform(kr, (DOUT, 1), jnp.float32, -lim_a, lim_a)
        return {'X': X, 'A': A, 'W': W, 'b': b, 'a_s': a_s, 'a_r': a_r}
    _L0_gnn_all = _L0_gnn_setup()
    _L0_gnn_in = {k: v for k, v in _L0_gnn_all.items() if k in ('W', 'b', 'a_s', 'a_r', )}
    del _L0_gnn_all

    def _L1_gnn_setup():
        import jax, jax.numpy as jnp
        import numpy as np
        N = 8192
        F_IN = 128
        F_OUT = 128
        BLOCK = 64

        def _graph_pool(out, adj):
            neg = jnp.asarray(jnp.finfo(out.dtype).min, out.dtype)

            def body(_, adj_blk):
                masked = jnp.where(adj_blk[:, :, None] != 0, out[None, :, :], neg)
                return (None, jnp.max(masked, axis=1))
            _, blocks = jax.lax.scan(body, None, adj.reshape(N // BLOCK, BLOCK, N))
            return blocks.reshape(N, out.shape[-1])
        key = jax.random.key(seed)
        k_in, k_adj, k_w, k_b = jax.random.split(key, 4)
        x = jax.random.normal(k_in, (N, F_IN), dtype=jnp.float32)
        adj = (jax.random.uniform(k_adj, (N, N)) < 0.01).astype(jnp.float32)
        adj = adj.at[jnp.arange(N), jnp.arange(N)].set(1.0)
        stdv = 1.0 / np.sqrt(F_OUT)
        weight = jax.random.uniform(k_w, (F_IN, F_OUT), minval=-stdv, maxval=stdv, dtype=jnp.float32)
        bias = jax.random.uniform(k_b, (F_OUT,), minval=-stdv, maxval=stdv, dtype=jnp.float32)
        return {'input': x, 'adj': adj, 'weight': weight, 'bias': bias}
    _L1_gnn_all = _L1_gnn_setup()
    _L1_gnn_in = {k: v for k, v in _L1_gnn_all.items() if k in ('weight', 'bias', )}
    del _L1_gnn_all

    return {
        "x": x,
        "adj": adj,
        "L0_gnn_W": _L0_gnn_in["W"],
        "L0_gnn_b": _L0_gnn_in["b"],
        "L0_gnn_a_s": _L0_gnn_in["a_s"],
        "L0_gnn_a_r": _L0_gnn_in["a_r"],
        "L1_gnn_weight": _L1_gnn_in["weight"],
        "L1_gnn_bias": _L1_gnn_in["bias"],
    }

def reference(x, adj, L0_gnn_W, L0_gnn_b, L0_gnn_a_s, L0_gnn_a_r, L1_gnn_weight, L1_gnn_bias):
    import jax
    import jax.numpy as jnp
    def _L0_gnn_ref(X, A, W, b, a_s, a_r):
        import jax, jax.numpy as jnp
        import numpy as np
        N, DIN, DOUT = (8192, 128, 128)
        NEG = -9000000000000000.0
        ALPHA = 0.2
        H = X @ W.T + b
        s = H @ a_s
        r = H @ a_r
        e = jax.nn.leaky_relu(A * s + A * r.T, negative_slope=ALPHA)
        masked = jnp.where(A > 0, e, NEG)
        att = jax.nn.softmax(masked, axis=1)
        H_out = att @ H
        return H_out

    def _L1_gnn_ref(input, adj, weight, bias):
        import jax, jax.numpy as jnp
        import numpy as np
        N = 8192
        F_IN = 128
        F_OUT = 128
        BLOCK = 64

        def _graph_pool(out, adj):
            neg = jnp.asarray(jnp.finfo(out.dtype).min, out.dtype)

            def body(_, adj_blk):
                masked = jnp.where(adj_blk[:, :, None] != 0, out[None, :, :], neg)
                return (None, jnp.max(masked, axis=1))
            _, blocks = jax.lax.scan(body, None, adj.reshape(N // BLOCK, BLOCK, N))
            return blocks.reshape(N, out.shape[-1])
        h = input @ weight
        out = jnp.maximum(adj @ h + bias, 0.0)
        return _graph_pool(out, adj)

    h = jnp.maximum(_layernorm(x, axis=-1), 0.0)
    x = x + _L0_gnn_ref(h, adj, L0_gnn_W, L0_gnn_b, L0_gnn_a_s, L0_gnn_a_r)
    h = jnp.maximum(_layernorm(x, axis=-1), 0.0)
    x = x + _L1_gnn_ref(h, adj, L1_gnn_weight, L1_gnn_bias)
    return x


_drawn_inputs = setup_inputs


def setup_inputs(seed=0):
    import zlib

    import numpy as np

    out = dict(_drawn_inputs(seed))
    spreads = {'L0_gnn_b': (0.0, 0.1)}
    factors = {'L0_gnn_a_s': 36.547, 'L1_gnn_bias': 28.415}
    for name, (base, spread) in spreads.items():
        noise = np.random.default_rng([zlib.crc32(name.encode()), seed]).standard_normal(out[name].shape)
        drawn = base * np.exp(spread * noise) if base else spread * noise
        out[name] = jnp.asarray(drawn.astype(out[name].dtype))
    for name, factor in factors.items():
        out[name] = (out[name] * factor).astype(out[name].dtype)
    return out
```

```python
from contextlib import ExitStack

import concourse.bass as bass
from concourse import mybir

F32, BF16 = mybir.dt.float32, mybir.dt.bfloat16
I32, U32 = mybir.dt.int32, mybir.dt.uint32
ALU, ACT, AX = mybir.AluOpType, mybir.ActivationFunctionType, mybir.AxisListType

P = 128
N = 8192
D = 128
T = N // P
WORDS = 1024
PLANES = N // WORDS
BANK = 512
VSCALE = 512.0
GROUP = 4
WGROUPS = 8
WSLOTS = GROUP * WGROUPS
LIGHT = 48
LIGHT_STORE = 2 * WSLOTS
NARROW = 16
PITCH = 132
ROWLEN = N
EPS = 1e-5
ALPHA = 0.2
MASKED = -9e15
UNUSED = -1e30
LOWEST = -3.4028234663852886e38


def build(nc, x, adj, W0, b0, a_s, a_r, W1, b1, out):
    ctx = ExitStack()
    with ctx:
        def sb(name, shape, dt=F32):
            return ctx.enter_context(nc.sbuf_tensor(name, shape, dt))

        def ps(name, shape, dt=F32):
            return ctx.enter_context(nc.psum_tensor(name, shape, dt))

        def sem(name):
            return ctx.enter_context(nc.semaphore(name))

        h_table = nc.dram_tensor("h_table", [N + 1, D + 1], F32).ap()
        y_table = nc.dram_tensor("y_table", [N + 1, D], F32).ap()
        p_table = nc.dram_tensor("p_table", [N + 1, D], F32).ap()
        lists = nc.dram_tensor("lists", [T, P, ROWLEN], U32).ap()

        xs = sb("xs", [P, T, D])
        a_buf = sb("a_buf", [P, 2, N])
        a_half = a_buf[:].bitcast(BF16).rearrange("p b (n two) -> p b n two", two=2)
        gathered = sb("gathered", [P, 2 * WSLOTS, PITCH])
        slots_in = sb("slots_in", [P, 2, WSLOTS], U32)
        ident = sb("ident", [P, P])
        bit_ident = sb("bit_ident", [P, PLANES, P], BF16)
        ones_bf = sb("ones_bf", [P, P], BF16)
        word_no = sb("word_no", [P, WORDS], BF16)
        word_i = sb("word_i", [P, WORDS], I32)
        zeros_bf = sb("zeros_bf", [P, BANK], BF16)
        bit_mask = sb("bit_mask", [P, PLANES], I32)
        bit_node = sb("bit_node", [P, PLANES])
        chunk_base = sb("chunk_base", [P, PLANES])
        iota8 = sb("iota8", [P, PLANES], I32)
        ones_row = sb("ones_row", [P, P])
        w0_sb = sb("w0_sb", [P, D])
        w0_rhs = sb("w0_rhs", [P, D + 2])
        w0_aug = sb("w0_aug", [P, D + 2])
        b0_col = sb("b0_col", [P, 1])
        b0_rep = sb("b0_rep", [P, P])
        b0_aug = sb("b0_aug", [P, D + 2])
        w1_sb = sb("w1_sb", [P, D])
        b1_rep = sb("b1_rep", [P, D])
        stats = sb("stats", [P, T, 6])
        mv = sb("mv", [P, T, 2])
        eps_col = sb("eps_col", [P, 1])
        rstd = sb("rstd", [P, T])
        hn = [sb(f"hn{i}", [P, D]) for i in range(2)]
        hT = [sb(f"hT{i}", [P, P]) for i in range(2)]
        stage = [sb(f"stage{i}", [P, D + 1]) for i in range(2)]
        s_col = sb("s_col", [P, T])
        neutral = sb("neutral", [1, D + 1])
        deg8 = sb("deg8", [P, 1])
        deg_junk = sb("deg_junk", [P, N], BF16)
        meta_deg = sb("meta_deg", [1, T], I32)
        meta_groups = sb("meta_groups", [1, T], I32)
        chunk_rounds = sb("chunk_rounds", [1, PLANES], I32)
        mdeg = sb("mdeg", [1, 2])
        V = sb("V", [P, WORDS])
        words = sb("words", [P, LIGHT])
        words_i = sb("words_i", [P, LIGHT], I32)
        words_no = sb("words_no", [P, LIGHT], I32)
        bits = sb("bits", [P, LIGHT, PLANES], I32)
        node = sb("node", [P, LIGHT, PLANES])
        found = sb("found", [P, LIGHT])
        top8 = sb("top8", [P, 8])
        top8n = sb("top8n", [P, 8])
        cdeg = sb("cdeg", [P, 1])
        slots_out = sb("slots_out", [P, WORDS], U32)
        e_raw = sb("e_raw", [P, WSLOTS])
        e_sc = sb("e_sc", [P, WSLOTS])
        prob = sb("prob", [P, WSLOTS])
        m_old, m_win, m_new, m_neg, alpha, lsum, lwin, linv = (
            sb(n, [P, 1]) for n in ("m_old", "m_win", "m_new", "m_neg", "alpha", "lsum", "lwin", "linv"))
        acc = sb("acc", [P, D])
        part = sb("part", [P, D])
        acc4 = sb("acc4", [P, GROUP, D])
        stage2 = sb("stage2", [P, 2, D])

        psV = ps("psV", [P, WORDS])
        psA = ps("psA", [P, BANK])
        psT = [ps(f"psT{i}", [P, BANK])[:, 0:P] for i in range(2)]
        psH = [ps(f"psH{i}", [P, BANK])[:, 0:D + 2] for i in range(2)]
        psM = ps("psM", [P, BANK])

        s_held = sem("s_held")
        s_xin, s_w, s_b1 = sem("s_xin"), sem("s_w"), sem("s_b1")
        s_c0, s_c1, s_c2, s_const = sem("s_c0"), sem("s_c1"), sem("s_c2"), sem("s_const")
        s_waug = sem("s_waug")
        s_waug_sb = sem("s_waug_sb")
        s_var = [sem(f"s_var{l}") for l in range(2)]
        s_std = [sem(f"s_std{l}") for l in range(2)]
        s_hn = [sem(f"s_hn{l}") for l in range(2)]
        s_tr = [sem(f"s_tr{l}") for l in range(2)]
        s_hT = [sem(f"s_hT{l}") for l in range(2)]
        s_mm = [sem(f"s_mm{l}") for l in range(2)]
        s_row = [sem(f"s_row{l}") for l in range(2)]
        s_colsum, s_neutral = sem("s_colsum"), sem("s_neutral")
        s_tab = [[sem(f"s_tab{l}{i}") for i in range(2)] for l in range(2)]
        s_tabn = sem("s_tabn")
        s_table = sem("s_table")
        s_a = [sem("s_a0"), sem("s_a1")]
        s_deg, s_degT, s_meta, s_groups = sem("s_deg"), sem("s_degT"), sem("s_meta"), sem("s_groups")
        s_fill, s_drained, s_afree = sem("s_fill"), sem("s_drained"), sem("s_afree")
        s_cdeg, s_cT, s_cm = sem("s_cdeg"), sem("s_cT"), sem("s_cm")
        s_slots, s_stored, s_listed = sem("s_slots"), sem("s_stored"), sem("s_listed")
        s_load = [sem(f"s_load{f}") for f in range(3)]
        s_rows = [[sem(f"s_rows{f}{i}") for i in range(2)] for f in range(3)]
        s_free = [sem(f"s_free{f}") for f in range(3)]
        s_e, s_p, s_scaled, s_acc, s_accread, s_x1 = (
            sem("s_e"), sem("s_p"), sem("s_scaled"), sem("s_acc"), sem("s_accread"), sem("s_x1"))
        s_sum, s_sumread, s_prow, s_prowfree, s_pst = (
            sem("s_sum"), sem("s_sumread"), sem("s_prow"), sem("s_prowfree"), sem("s_pst"))
        s_orow, s_orowfree, s_ost = sem("s_orow"), sem("s_orowfree"), sem("s_ost")

        def register(eng, name):
            r = eng.alloc_register(name)
            eng.reg_mov(r, 0)
            return r

        def bump(eng, r, n=1):
            eng.reg_add(r, r, n)

        def bounded(eng, value, least, most):
            r = eng.alloc_register(f"bounded{nc.next_id()}")
            eng.reg_mov(r, value)
            return eng.snap(r, min_val=least, max_val=most)

        def groups_here(eng, rest):
            left, most, r = (eng.alloc_register(f"here{nc.next_id()}") for _ in range(3))
            eng.reg_mov(left, rest)
            eng.reg_alu(most, left, WGROUPS, ALU.min)
            eng.reg_alu(r, most, 1, ALU.max)
            return eng.snap(r, min_val=1, max_val=WGROUPS)

        def tile(eng, t):
            return bounded(eng, t, 0, T - 1)

        def windows(eng, name, body, before=None, after=None, tiles=None):
            count = register(eng, f"{name}_k")
            with eng.Fori(0, T) as t:
                if before is not None:
                    before(t)
                groups = eng.value_load(meta_groups[0:1, bass.ds(t, 1)], min_val=1, max_val=ROWLEN // GROUP)
                with eng.Fori(0, (groups + (WGROUPS - 1)) // WGROUPS) as w:
                    body(t, w, eng.snap(count, min_val=0, max_val=1 << 17), groups - w * WGROUPS, groups)
                    bump(eng, count)
                if after is not None:
                    after(t)

        def slot_at(k, g):
            return (k % 2) * WSLOTS + g * GROUP

        def hold(eng, semaphore, value):
            eng.wait_ge(semaphore, value)
            eng.sem_inc(s_held, 1)

        def gathered_counts(eng, phase):
            return [register(eng, f"rows{phase}{b}_{nc.next_id()}") for b in range(2)]

        def wait_gathered(eng, phase, counts, n, groups):
            for b in range(2):
                with (eng.If(n % 2 == 1) if b == 0 else eng.Else()):
                    eng.reg_add(counts[b], counts[b], groups * (GROUP * 16))
                    hold(eng, s_rows[phase][b], eng.snap(counts[b], min_val=0, max_val=1 << 24))

        block = ctx.enter_context(nc.Block())

        @block.sync
        def _(sp):
            sp.dma_start(xs[:, :, :], x.rearrange("(t p) c -> p t c", p=P)).then_inc(s_xin, 16)
            sp.dma_start(w0_sb[:], W0).then_inc(s_w, 16)
            sp.dma_start(w0_rhs[:, D:D + 1], a_s).then_inc(s_w, 16)
            sp.dma_start(w0_rhs[:, D + 1:D + 2], a_r).then_inc(s_w, 16)
            sp.dma_start(b0_col[:], b0.rearrange("(p a) -> p a", a=1)).then_inc(s_w, 16)
            sp.dma_start(w1_sb[:], W1).then_inc(s_w, 16)
            sp.dma_start(b1_rep[:], b1.rearrange("(a n) -> a n", a=1).to_broadcast([P, D])).then_inc(s_b1, 16)
            for u in range(2):
                sp.dma_start(a_buf[:, u, :], adj[u * P:(u + 1) * P, :]).then_inc(s_a[u], 16)

            def store_table(layer, table, width):
                with sp.Fori(0, T // 2) as tp:
                    for u in range(2):
                        t = 2 * tp + u
                        sp.wait_ge(s_row[layer], t + 1)
                        sp.dma_start(table[bass.ds(t * P + 1, P), :], stage[u][:, 0:width]).then_inc(
                            s_tab[layer][u], 16)
                for u in range(2):
                    sp.wait_ge(s_tab[layer][u], 16 * (T // 2))

            store_table(0, h_table, D + 1)
            sp.wait_ge(s_neutral, 3)
            sp.dma_start(h_table[0:1, :], neutral[0:1, :]).then_inc(s_tabn, 16)
            sp.wait_ge(s_tabn, 16)
            sp.sem_inc(s_table, 1)

            stores = register(sp, "sp_stores")
            offset = register(sp, "sp_offset")
            spare = register(sp, "sp_spare")

            def store_lists(t):
                sp.wait_ge(s_meta, t + 1)
                deg = sp.value_load(meta_deg[0:1, bass.ds(t, 1)], min_val=1, max_val=N)
                with sp.If(deg <= LIGHT):
                    n = sp.snap(stores, min_val=0, max_val=1 << 12)
                    sp.wait_ge(s_slots, n + 1)
                    sp.dma_start(lists[bass.ds(t, 1), :, 0:LIGHT_STORE].rearrange("a p n -> (a p) n"),
                                 slots_out[:, 0:LIGHT_STORE]).then_inc(s_stored, 16)
                    bump(sp, stores)
                with sp.Else():
                    sp.reg_mov(offset, 0)
                    with sp.Fori(0, PLANES) as c:
                        n = sp.snap(stores, min_val=0, max_val=1 << 12)
                        sp.wait_ge(s_slots, n + 1)
                        at = sp.snap(offset, min_val=0, max_val=N - WORDS)
                        sp.dma_start(lists[bass.ds(t, 1), :, bass.ds(at, WORDS)].rearrange("a p n -> (a p) n"),
                                     slots_out[:, :]).then_inc(s_stored, 16)
                        sp.wait_ge(s_stored, (n + 1) * 16)
                        r = sp.value_load(chunk_rounds[0:1, bass.ds(c, 1)], min_val=0, max_val=WORDS // 8)
                        sp.reg_add(offset, offset, r * 8)
                        bump(sp, stores)
                n = sp.snap(stores, min_val=0, max_val=1 << 12)
                hold(sp, s_stored, n * 16)
                sp.sem_inc(s_listed, 1)

            store_lists(0)
            with sp.Fori(0, T // 2) as tp:
                for u in range(2):
                    t = 2 * tp + u
                    with sp.If(t < T - 2):
                        sp.wait_ge(s_afree, t + 1)
                        sp.wait_ge(s_deg, t + 1)
                        sp.dma_start(a_buf[:, u, :], adj[bass.ds(tile(sp, t + 2) * P, P), :]).then_inc(s_a[u], 16)
                    with sp.If(t < T - 1):
                        store_lists(tile(sp, t + 1))
                        bump(sp, spare)

            store_table(1, y_table, D)
            sp.wait_ge(s_neutral, 4)
            sp.dma_start(y_table[0:1, :], neutral[0:1, 0:D]).then_inc(s_tabn, 16)
            sp.wait_ge(s_tabn, 32)
            sp.sem_inc(s_table, 1)

            with sp.Fori(0, T) as t:
                sp.wait_ge(s_prow, t + 1)
                sp.dma_start(p_table[bass.ds(t * P + 1, P), :],
                             stage2[:, bass.ds(t % 2, 1), :].rearrange("p a d -> p (a d)")).then_inc(s_pst, 16)
                sp.wait_ge(s_pst, (t + 1) * 16)
                sp.sem_inc(s_prowfree, 1)
            sp.wait_ge(s_neutral, 5)
            sp.dma_start(p_table[0:1, :], neutral[0:1, 0:D]).then_inc(s_tabn, 16)
            sp.wait_ge(s_tabn, 48)
            sp.sem_inc(s_table, 1)

            with sp.Fori(0, T) as t:
                sp.wait_ge(s_orow, t + 1)
                sp.dma_start(out[bass.ds(t * P, P), :],
                             stage2[:, bass.ds(t % 2, 1), :].rearrange("p a d -> p (a d)")).then_inc(s_ost, 16)
                sp.wait_ge(s_ost, (t + 1) * 16)
                sp.sem_inc(s_orowfree, 1)

        @block.gpsimd
        def _(pool):
            pool.memset(ident[:], 0.0).then_inc(s_c0, 1)
            pool.memset(w0_rhs[:, 0:D], 0.0).then_inc(s_c0, 1)
            pool.wait_ge(s_c0, 2)
            for m in (ident[:], w0_rhs[:, 0:D]):
                pool.affine_select(out=m, in_=m, compare_op=ALU.not_equal, fill=1.0, base=0,
                                   pattern=[[-1, P]], channel_multiplier=1).then_inc(s_c1, 1)
            pool.iota(word_i[:], pattern=[[1, WORDS]], base=0, channel_multiplier=0).then_inc(s_c1, 1)
            pool.iota(iota8[:], pattern=[[1, PLANES]], base=0, channel_multiplier=0).then_inc(s_c1, 1)
            pool.memset(ones_row[:], 1.0).then_inc(s_c1, 1)
            pool.memset(gathered[:], 0.0).then_inc(s_c2, 1)
            pool.wait_ge(s_c2, 1)

            for phase, (table, width) in enumerate(((h_table, D + 1), (y_table, D), (p_table, D))):
                pool.wait_ge(s_table, phase + 1)

                def before(t, phase=phase):
                    if phase == 0:
                        pool.wait_ge(s_groups, t + 1)

                def gather(t, w, k, rest, groups, phase=phase, table=table, width=width):
                    pool.wait_ge(s_load[phase], (k + 1) * 16)
                    pool.wait_ge(s_free[phase], k + 1)
                    for b in range(2):
                        def rows(g, b=b):
                            for j in range(g * GROUP, (g + 1) * GROUP):
                                pool.indirect_dma_start(
                                    gathered[:, b * WSLOTS + j, 0:width], None, table,
                                    bass.IndirectOffsetOnAxis(slots_in[:, b, j:j + 1], 0),
                                    bounds_check=N, oob_is_err=False).then_inc(s_rows[phase][b], 16)

                        with (pool.If(k % 2 == 0) if b == 0 else pool.Else()):
                            rows(0)
                            for g in range(1, WGROUPS):
                                with pool.If(rest > g):
                                    rows(g)

                windows(pool, f"pool{phase}", gather, before)

        @block.scalar
        def _(act):
            spare = register(act, "act_spare")

            def norm(layer):
                act.wait_ge(s_var[layer], 1)
                act.activation(rstd[:], mv[:, :, 1], ACT.Sqrt, bias=eps_col[:, 0:1]).then_inc(s_std[layer], 1)
                with act.Fori(0, T // 2) as tp:
                    for u in range(2):
                        t = 2 * tp + u
                        act.wait_ge(s_tr[layer], t + 1)
                        act.activation(hT[u][:], psT[u][:], ACT.Relu).then_inc(s_hT[layer], 1)

            norm(0)

            def count_degrees(t, u):
                act.wait_ge(s_a[u], (t // 2 + 1) * 16)
                act.wait_ge(s_degT, t)
                act.activation(deg_junk[:], a_buf[:, u, :], ACT.Copy, accum_out=deg8[:, 0:1]).then_inc(s_deg, 1)

            def load_window(phase, t, w, k):
                act.dma_start(slots_in[:, bass.ds(k % 2, 1), :].rearrange("p a n -> p (a n)"),
                              lists[bass.ds(t, 1), :, bass.ds(w * WSLOTS, WSLOTS)].rearrange(
                                  "a p n -> (a p) n")).then_inc(s_load[phase], 16)

            last_groups = register(act, "act_last")

            def load_next(phase, counts, t, w, k, rest):
                with act.If(k > 0):
                    wait_gathered(act, phase, counts, k, act.snap(last_groups, min_val=0, max_val=WGROUPS))
                    bump(act, spare)
                act.wait_ge(s_load[phase], (k + 1) * 16)
                with act.If(rest > WGROUPS):
                    load_window(phase, t, bounded(act, w + 1, 1, N // WSLOTS - 1), k + 1)
                with act.Else():
                    with act.If(t < T - 1):
                        if phase == 0:
                            act.wait_ge(s_listed, t + 2)
                        load_window(phase, tile(act, t + 1), 0, k + 1)
                    bump(act, spare)
                act.reg_mov(last_groups, groups_here(act, rest))

            count_degrees(0, 0)
            count_degrees(1, 1)
            act.wait_ge(s_listed, 1)
            act.dma_start(slots_in[:, 0, :], lists[0, :, 0:WSLOTS]).then_inc(s_load[0], 16)

            count = register(act, "act_k")
            counts = gathered_counts(act, 0)
            with act.Fori(0, T // 2) as tp:
                for u in range(2):
                    t = 2 * tp + u
                    with act.If(t < T - 2):
                        count_degrees(tile(act, t + 2), u)
                    act.wait_ge(s_groups, t + 1)
                    groups = act.value_load(meta_groups[0:1, bass.ds(t, 1)], min_val=1, max_val=ROWLEN // GROUP)
                    with act.Fori(0, (groups + (WGROUPS - 1)) // WGROUPS) as w:
                        k = act.snap(count, min_val=0, max_val=1 << 17)
                        load_next(0, counts, t, w, k, groups - w * WGROUPS)
                        act.wait_ge(s_e, k + 1)
                        act.activation(prob[:], e_sc[:], ACT.Exp, bias=m_neg[:, 0:1], accum_out=lwin[:, 0:1])
                        act.activation(alpha[:], m_old[:], ACT.Exp, bias=m_neg[:, 0:1]).then_inc(s_p, 1)
                        bump(act, count)

            norm(1)
            for phase in (1, 2):
                act.dma_start(slots_in[:, 0, :], lists[0, :, 0:WSLOTS]).then_inc(s_load[phase], 16)

                counts = gathered_counts(act, phase)

                def feed(t, w, k, rest, groups, phase=phase, counts=counts):
                    load_next(phase, counts, t, w, k, rest)

                windows(act, f"act{phase}", feed)
                if phase == 1:
                    act.wait_ge(s_table, 3)

        @block.tensor
        def _(pe):
            spare = register(pe, "pe_spare")
            pe.wait_ge(s_w, 80)
            pe.wait_ge(s_const, 1)
            pe.matmul(psH[0][:], w0_sb[:], w0_rhs[:], start=True, stop=True)
            pe.matmul(psH[1][:], b0_rep[:], w0_rhs[:], start=True, stop=True).then_inc(s_waug, 1)
            pe.wait_ge(s_waug_sb, 1)

            def norm(layer, weights, width):
                def transpose(t, u):
                    pe.wait_ge(s_hn[layer], t + 1)
                    pe.transpose(psT[u][:], hn[u][:], ident[:]).then_inc(s_tr[layer], 1)

                transpose(0, 0)
                with pe.Fori(0, T // 2) as tp:
                    for u in range(2):
                        t = 2 * tp + u
                        with pe.If(t < T - 1):
                            transpose(tile(pe, t + 1), 1 - u)
                        pe.wait_ge(s_hT[layer], t + 1)
                        pe.wait_ge(s_row[layer], t)
                        pe.matmul(psH[u][:, 0:width], hT[u][:], weights, start=True, stop=True).then_inc(
                            s_mm[layer], 1)

            norm(0, w0_aug[:], D + 2)
            pe.wait_ge(s_colsum, 1)
            pe.matmul(psM[0:1, 0:D], ones_row[:, 0:1], acc[:], start=True, stop=True).then_inc(s_colsum, 1)
            pe.wait_ge(s_neutral, 3)

            fills = register(pe, "pe_fills")
            heavy_chunks = register(pe, "pe_chunks")

            def fill_wait():
                n = pe.snap(fills, min_val=0, max_val=1 << 12)
                pe.wait_ge(s_drained, n)
                bump(pe, fills)

            def number_words():
                for h in range(2):
                    last = pe.matmul(psV[:, h * BANK:(h + 1) * BANK], ones_bf[:],
                                     word_no[:, h * BANK:(h + 1) * BANK], start=False, stop=True)
                return last

            def degrees(t):
                pe.wait_ge(s_deg, t + 1)
                pe.wait_ge(s_meta, t)
                pe.matmul(psM[0:1, 0:P], deg8[:], ident[:], start=True, stop=True).then_inc(s_degT, 1)

            def load_degree(t):
                pe.wait_ge(s_meta, t + 1)
                return pe.value_load(meta_deg[0:1, bass.ds(t, 1)], min_val=1, max_val=N)

            def pack_light(t, u):
                with pe.If(load_degree(t) <= LIGHT):
                    fill_wait()
                    pe.wait_ge(s_a[u], (t // 2 + 1) * 16)
                    for h in range(2):
                        for k in range(PLANES):
                            at = k * WORDS + h * BANK
                            pe.matmul(psV[:, h * BANK:(h + 1) * BANK], bit_ident[:, k, :],
                                      a_half[:, u, at:at + BANK, 1], start=(k == 0), stop=False)
                    number_words().then_inc(s_fill, 1)
                    pe.drain().then_inc(s_afree, 1)
                    bump(pe, spare)

            def pack_heavy(t, u):
                with pe.If(load_degree(t) > LIGHT):
                    hold(pe, s_a[u], (t // 2 + 1) * 16)
                    with pe.Fori(0, PLANES) as c:
                        fill_wait()
                        for h in range(2):
                            pe.matmul(psV[:, h * BANK:(h + 1) * BANK], bit_ident[:, 0, :],
                                      a_half[:, u, bass.ds(c * WORDS + h * BANK, BANK), 1],
                                      start=True, stop=False)
                        number_words().then_inc(s_fill, 1)
                        bump(pe, heavy_chunks)
                        n = pe.snap(heavy_chunks, min_val=0, max_val=1 << 12)
                        pe.wait_ge(s_cdeg, n)
                        pe.matmul(psH[1][0:1, 0:P], cdeg[:], ident[:], start=True, stop=True).then_inc(s_cT, 1)
                        bump(pe, spare)
                    pe.drain().then_inc(s_afree, 1)
                    bump(pe, spare)

            degrees(0)
            pack_light(0, 0)
            pack_heavy(0, 0)
            degrees(1)
            pack_light(1, 1)

            def add_groups(n, k):
                with pe.Fori(0, n) as g:
                    pe.matmul(psA[:].rearrange("p (j d) -> p j d", d=D), ident[:],
                              gathered[:, bass.ds(slot_at(k, g), GROUP), 0:D],
                              start=False, stop=False)

            count = register(pe, "pe_k")
            with pe.Fori(0, T // 2) as tp:
                for u in range(2):
                    t = 2 * tp + u
                    with pe.If(t < T - 1):
                        pack_heavy(tile(pe, t + 1), 1 - u)
                        bump(pe, spare)
                    with pe.If(t < T - 2):
                        ahead = tile(pe, t + 2)
                        degrees(ahead)
                        pack_light(ahead, u)
                        bump(pe, spare)
                    pe.wait_ge(s_groups, t + 1)
                    groups = pe.value_load(meta_groups[0:1, bass.ds(t, 1)], min_val=1, max_val=ROWLEN // GROUP)
                    with pe.Fori(0, (groups + (WGROUPS - 1)) // WGROUPS) as w:
                        k = pe.snap(count, min_val=0, max_val=1 << 17)
                        pe.wait_ge(s_accread, k)
                        pe.matmul(psA[:], ones_bf[:], zeros_bf[:], start=True, stop=False)
                        pe.wait_ge(s_scaled, k + 1)
                        add_groups(groups_here(pe, groups - w * WGROUPS), k)
                        pe.matmul(psA[:], ones_bf[:], zeros_bf[:], start=False, stop=True).then_inc(s_acc, 1)
                        pe.drain().then_inc(s_free[0], 1)
                        bump(pe, count)

            norm(1, w1_sb[:], D)

            rows_seen = gathered_counts(pe, 1)

            def begin(t):
                pe.wait_ge(s_sumread, t)
                pe.matmul(psA[:], ones_bf[:], zeros_bf[:], start=True, stop=False)

            def add_window(t, w, k, rest, groups):
                n = groups_here(pe, rest)
                wait_gathered(pe, 1, rows_seen, k + 1, n)
                add_groups(n, k)
                pe.drain().then_inc(s_free[1], 1)

            def end(t):
                pe.matmul(psA[:], ones_bf[:], zeros_bf[:], start=False, stop=True).then_inc(s_sum, 1)

            windows(pe, "pe1", add_window, begin, end)

        @block.vector
        def _(dve):
            spare = register(dve, "dve_spare")
            dve.memset(eps_col[:], EPS)
            dve.memset(ones_bf[:], 1.0)
            dve.memset(zeros_bf[:], 0.0)
            for f in range(3):
                dve.sem_inc(s_free[f], 2)
            dve.sem_inc(s_prowfree, 2)
            dve.sem_inc(s_orowfree, 2)
            dve.wait_ge(s_c1, 5)
            for k in range(PLANES):
                dve.tensor_scalar(bit_ident[:, k, :], ident[:], float(2 ** (k + 1)), None, ALU.mult)
                dve.memset(bit_mask[:, k:k + 1], WORDS << k)
            dve.tensor_scalar(bit_node[:], iota8[:], float(WORDS), 1.0, ALU.mult, ALU.add)
            dve.tensor_scalar(chunk_base[:], iota8[:], float(WORDS), float(1 - WORDS), ALU.mult, ALU.add)
            hi, lo = bits[:].rearrange("p a b -> p (a b)"), node[:].rearrange("p a b -> p (a b)")
            for at in range(0, WORDS, LIGHT * PLANES):
                n = min(LIGHT * PLANES, WORDS - at)
                dve.drain()
                dve.tensor_scalar(hi[:, 0:n], word_i[:, at:at + n], WORDS - 8, None, ALU.bitwise_and)
                dve.drain()
                dve.tensor_scalar(V[:, at:at + n], hi[:, 0:n], 1.0 / VSCALE, None, ALU.mult)
                dve.drain()
                dve.tensor_scalar(hi[:, 0:n], word_i[:, at:at + n], 7, None, ALU.bitwise_and)
                dve.tensor_scalar(V[:, at:at + n], V[:, at:at + n], ident[:, 0:1], None, ALU.mult)
                dve.drain()
                dve.tensor_scalar(lo[:, 0:n], hi[:, 0:n], 1.0 / VSCALE, None, ALU.mult)
                dve.drain()
                dve.scalar_tensor_tensor(word_no[:, at:at + n], lo[:, 0:n], ident[:, 1:2], V[:, at:at + n],
                                         ALU.mult, ALU.add)
            dve.wait_ge(s_w, 80)
            dve.tensor_scalar(b0_rep[:], ones_row[:], b0_col[:, 0:1], None, ALU.mult)
            dve.drain().then_inc(s_const, 1)
            dve.wait_ge(s_waug, 1)
            dve.tensor_copy(w0_aug[:], psH[0][:])
            dve.tensor_copy(b0_aug[:], psH[1][:])
            dve.drain().then_inc(s_waug_sb, 1)

            def norm(layer):
                with dve.Fori(0, T) as t:
                    dve.bn_stats(stats[:, bass.ds(t, 1), :].rearrange("p a c -> p (a c)"),
                                 xs[:, bass.ds(t, 1), :].rearrange("p a c -> p (a c)"))
                dve.drain()
                for t in range(T):
                    dve.bn_aggr(mv[:, t, :], stats[:, t, :])
                dve.drain().then_inc(s_var[layer], 1)
                dve.wait_ge(s_std[layer], 1)
                dve.reciprocal(rstd[:], rstd[:])
                dve.drain()

                def normalize(t, u):
                    dve.tensor_scalar(hn[u][:], xs[:, bass.ds(t, 1), :].rearrange("p a c -> p (a c)"),
                                      mv[:, bass.ds(t, 1), 0], rstd[:, bass.ds(t, 1)],
                                      ALU.subtract, ALU.mult).then_inc(s_hn[layer], 1)

                normalize(0, 0)
                with dve.Fori(0, T // 2) as tp:
                    for u in range(2):
                        t = 2 * tp + u
                        with dve.If(t < T - 1):
                            normalize(tile(dve, t + 1), 1 - u)
                        dve.wait_ge(s_mm[layer], t + 1)
                        dve.wait_ge(s_tab[layer][u], tp * 16)
                        if layer == 0:
                            dve.tensor_tensor(s_col[:, bass.ds(t, 1)], psH[u][:, D:D + 1], b0_aug[:, D:D + 1],
                                              ALU.add)
                            dve.tensor_tensor(stage[u][:, D:D + 1], psH[u][:, D + 1:D + 2],
                                              b0_aug[:, D + 1:D + 2], ALU.add)
                            dve.tensor_tensor(stage[u][:, 0:D], psH[u][:, 0:D], b0_aug[:, 0:D], ALU.add)
                            dve.drain()
                            with dve.If(t == 0):
                                dve.tensor_copy(acc[:], stage[u][:, 0:D])
                            with dve.Else():
                                dve.tensor_tensor(acc[:], acc[:], stage[u][:, 0:D], ALU.add)
                            dve.drain().then_inc(s_row[layer], 1)
                        else:
                            dve.tensor_copy(stage[u][:, 0:D], psH[u][:, 0:D]).then_inc(s_row[layer], 1)

            dve.wait_ge(s_xin, 16)
            norm(0)
            dve.drain().then_inc(s_colsum, 1)
            dve.wait_ge(s_colsum, 2)
            dve.tensor_scalar(neutral[0:1, 0:D], psM[0:1, 0:D], 1.0 / N, None, ALU.mult)
            dve.memset(neutral[0:1, D:D + 1], MASKED)
            dve.drain().then_inc(s_neutral, 3)

            fills = register(dve, "dve_fills")
            stores = register(dve, "dve_stores")
            chunks = register(dve, "dve_chunks")

            def meta(t):
                dve.wait_ge(s_degT, t + 1)
                dve.reduce_max(mdeg[0:1, 0:1], psM[0:1, 0:P], axis=AX.X)
                dve.drain()
                dve.tensor_scalar(meta_deg[0:1, bass.ds(t, 1)], mdeg[0:1, 0:1], 1.0, None, ALU.max)
                dve.drain()
                dve.tensor_scalar(meta_groups[0:1, bass.ds(t, 1)], meta_deg[0:1, bass.ds(t, 1)],
                                  float(GROUP - 1), None, ALU.add)
                dve.drain()
                dve.tensor_scalar(meta_groups[0:1, bass.ds(t, 1)], meta_groups[0:1, bass.ds(t, 1)],
                                  2, None, ALU.logical_shift_right)
                dve.drain().then_inc(s_meta, 1)

            def wait_fill():
                n = dve.snap(fills, min_val=0, max_val=1 << 12)
                dve.wait_ge(s_fill, n + 1)
                bump(dve, fills)

            def wait_stored():
                n = dve.snap(stores, min_val=0, max_val=1 << 12)
                dve.wait_ge(s_stored, n * 16)
                bump(dve, stores)

            def expand(n, deg):
                dve.tensor_scalar(words_i[:, 0:n], words[:, 0:n], VSCALE, None, ALU.mult)
                dve.drain()
                dve.tensor_scalar(words_no[:, 0:n], words_i[:, 0:n], WORDS - 1, None, ALU.bitwise_and)
                dve.tensor_tensor(bits[:, 0:n, :], words_i[:, 0:n].unsqueeze(2).to_broadcast([P, n, PLANES]),
                                  bit_mask[:].unsqueeze(1).to_broadcast([P, n, PLANES]), ALU.bitwise_and)
                dve.drain()
                dve.tensor_tensor(node[:, 0:n, :], words_no[:, 0:n].unsqueeze(2).to_broadcast([P, n, PLANES]),
                                  bit_node[:].unsqueeze(1).to_broadcast([P, n, PLANES]), ALU.add)
                dve.drain()
                flat = node[:, 0:n, :].rearrange("p a b -> p (a b)")
                dve.scalar_tensor_tensor(flat, bits[:, 0:n, :].rearrange("p a b -> p (a b)"), 0.0, flat,
                                         ALU.is_gt, ALU.mult)
                dve.drain()
                for r in range(0, n, 8):
                    def pull(r=r):
                        dve.max(found[:, r:r + 8], flat)
                        dve.drain()
                        if r + 8 < n:
                            dve.match_replace(flat, found[:, r:r + 8], flat, 0.0)
                            dve.drain()
                    if r == 0:
                        pull()
                    else:
                        with dve.If(deg > r):
                            pull()

            def extract_light(deg):
                dve.memset(words[:], 0.0)
                dve.memset(found[:], 0.0)
                wait_fill()
                dve.drain()
                dve.max(words[:, 0:8], psV[:])
                dve.drain()
                dve.match_replace(V[:], words[:, 0:8], psV[:], 0.0).then_inc(s_drained, 1)
                for r in range(8, LIGHT, 8):
                    with dve.If(deg > r):
                        dve.drain()
                        dve.max(words[:, r:r + 8], V[:])
                        if r + 8 < LIGHT:
                            dve.drain()
                            dve.match_replace(V[:], words[:, r:r + 8], V[:], 0.0)
                dve.drain()
                with dve.If(deg > NARROW):
                    expand(LIGHT, deg)
                    bump(dve, spare)
                with dve.Else():
                    expand(NARROW, deg)
                    bump(dve, spare)
                wait_stored()
                dve.tensor_copy(slots_out[:, 0:LIGHT], found[:])
                dve.memset(slots_out[:, LIGHT:LIGHT_STORE], 0)
                dve.drain().then_inc(s_slots, 1)

            def extract_heavy(t):
                groups = meta_groups[0:1, bass.ds(t, 1)]
                dve.memset(mdeg[0:1, 1:2], 0.0)
                with dve.Fori(0, PLANES) as c:
                    wait_fill()
                    dve.drain()
                    dve.tensor_scalar(V[:], psV[:], 2.0, 0.0, ALU.is_ge, ALU.add, accum_out=cdeg[:, 0:1])
                    dve.drain().then_inc(s_cdeg, 1)
                    dve.tensor_copy(V[:], psV[:]).then_inc(s_drained, 1)
                    wait_stored()
                    dve.memset(slots_out[:], 0)
                    bump(dve, chunks)
                    n = dve.snap(chunks, min_val=0, max_val=1 << 12)
                    dve.wait_ge(s_cT, n)
                    dve.reduce_max(mdeg[0:1, 0:1], psH[1][0:1, 0:P], axis=AX.X)
                    dve.drain()
                    rounds = chunk_rounds[0:1, bass.ds(c, 1)]
                    dve.tensor_scalar(rounds, mdeg[0:1, 0:1], 7.0, None, ALU.add)
                    dve.drain()
                    dve.tensor_scalar(rounds, rounds, 3, None, ALU.logical_shift_right)
                    dve.drain()
                    dve.scalar_tensor_tensor(mdeg[0:1, 1:2], rounds, 2.0, mdeg[0:1, 1:2], ALU.mult, ALU.add)
                    dve.drain().then_inc(s_cm, 1)
                    hold(dve, s_cm, n)
                    todo = dve.value_load(rounds, min_val=0, max_val=WORDS // 8)
                    with dve.If(todo > 0):
                        with dve.Fori(0, todo) as r:
                            dve.max(top8[:], V[:])
                            dve.drain()
                            dve.match_replace(V[:], top8[:], V[:], 0.0)
                            dve.tensor_scalar(top8n[:], top8[:], VSCALE, chunk_base[:, bass.ds(c, 1)],
                                              ALU.mult, ALU.add)
                            dve.drain()
                            dve.scalar_tensor_tensor(slots_out[:, bass.ds(r * 8, 8)], top8[:], 2.0, top8n[:],
                                                     ALU.is_ge, ALU.mult)
                            dve.drain()
                        bump(dve, spare)
                    dve.drain().then_inc(s_slots, 1)
                dve.tensor_scalar(groups, mdeg[0:1, 1:2], 1.0, None, ALU.max)
                dve.drain()

            def extract(t):
                dve.wait_ge(s_meta, t + 1)
                deg = dve.value_load(meta_deg[0:1, bass.ds(t, 1)], min_val=1, max_val=N)
                with dve.If(deg <= LIGHT):
                    extract_light(deg)
                    bump(dve, spare)
                with dve.Else():
                    extract_heavy(t)
                    bump(dve, spare)
                dve.drain().then_inc(s_groups, 1)

            count = register(dve, "dve_k")

            rows_seen = gathered_counts(dve, 0)

            def attend_window(t, k, rest):
                n = groups_here(dve, rest)
                dve.memset(e_raw[:], UNUSED)
                wait_gathered(dve, 0, rows_seen, k + 1, n)
                dve.drain()
                with dve.Fori(0, n) as g:
                    dve.tensor_scalar(e_raw[:, bass.ds(g * GROUP, GROUP)],
                                      gathered[:, bass.ds(slot_at(k, g), GROUP), D],
                                      s_col[:, bass.ds(t, 1)], None, ALU.add)
                dve.drain()
                dve.scalar_tensor_tensor(e_sc[:], e_raw[:], ALPHA, e_raw[:], ALU.mult, ALU.max)
                dve.drain()
                dve.reduce_max(m_win[:], e_sc[:], axis=AX.X)
                dve.drain()
                dve.tensor_tensor(m_new[:], m_win[:], m_old[:], ALU.max)
                dve.drain()
                dve.tensor_scalar(m_neg[:], m_new[:], -1.0, None, ALU.mult)
                dve.drain().then_inc(s_e, 1)
                dve.wait_ge(s_p, k + 1)
                dve.tensor_copy(m_old[:], m_new[:])
                dve.scalar_tensor_tensor(lsum[:], lsum[:], alpha[:, 0:1], lwin[:], ALU.mult, ALU.add)
                with dve.Fori(0, n) as g:
                    rows = gathered[:, bass.ds(slot_at(k, g), GROUP), 0:D]
                    dve.tensor_tensor(rows, rows, prob[:, bass.ds(g * GROUP, GROUP)].unsqueeze(2).to_broadcast(
                        [P, GROUP, D]), ALU.mult)
                dve.drain().then_inc(s_scaled, 1)
                dve.wait_ge(s_acc, k + 1)
                dve.tensor_reduce(part[:], psA[:].rearrange("p (j d) -> p d j", d=D), AX.X, ALU.add).then_inc(
                    s_accread, 1)
                dve.drain()
                dve.scalar_tensor_tensor(acc[:], acc[:], alpha[:, 0:1], part[:], ALU.mult, ALU.add)
                dve.drain()

            meta(0)
            extract(0)
            meta(1)
            with dve.Fori(0, T) as t:
                with dve.If(t < T - 1):
                    extract(tile(dve, t + 1))
                    bump(dve, spare)
                with dve.If(t < T - 2):
                    meta(tile(dve, t + 2))
                    bump(dve, spare)
                dve.memset(m_old[:], LOWEST)
                dve.memset(lsum[:], 0.0)
                dve.memset(acc[:], 0.0)
                groups = dve.value_load(meta_groups[0:1, bass.ds(t, 1)], min_val=1, max_val=ROWLEN // GROUP)
                with dve.Fori(0, (groups + (WGROUPS - 1)) // WGROUPS) as w:
                    attend_window(t, dve.snap(count, min_val=0, max_val=1 << 17), groups - w * WGROUPS)
                    bump(dve, count)
                dve.reciprocal(linv[:], lsum[:])
                dve.drain()
                row = xs[:, bass.ds(t, 1), :].rearrange("p a c -> p (a c)")
                dve.scalar_tensor_tensor(row, acc[:], linv[:, 0:1], row, ALU.mult, ALU.add)
                dve.drain()

            dve.memset(neutral[0:1, :], 0.0)
            norm(1)
            dve.drain().then_inc(s_neutral, 1)

            dve.wait_ge(s_b1, 16)
            with dve.Fori(0, T) as t:
                dve.wait_ge(s_sum, t + 1)
                dve.tensor_reduce(part[:], psA[:].rearrange("p (j d) -> p d j", d=D), AX.X, ALU.add).then_inc(
                    s_sumread, 1)
                dve.drain()
                dve.tensor_tensor(acc[:], part[:], b1_rep[:], ALU.add)
                dve.drain()
                dve.wait_ge(s_prowfree, t + 1)
                dve.tensor_scalar(stage2[:, bass.ds(t % 2, 1), :].rearrange("p a d -> p (a d)"), acc[:],
                                  0.0, None, ALU.max).then_inc(s_prow, 1)
            dve.wait_ge(s_tabn, 32)
            dve.memset(neutral[0:1, :], LOWEST)
            dve.drain().then_inc(s_neutral, 1)
            dve.wait_ge(s_table, 3)

            rows_max = gathered_counts(dve, 2)

            def start_max(t):
                dve.memset(acc4[:], LOWEST)
                dve.drain()

            def add_max(t, w, k, rest, groups):
                n = groups_here(dve, rest)
                wait_gathered(dve, 2, rows_max, k + 1, n)
                with dve.Fori(0, n) as g:
                    dve.tensor_tensor(acc4[:], acc4[:], gathered[:, bass.ds(slot_at(k, g), GROUP), 0:D], ALU.max)
                    dve.drain()
                dve.drain().then_inc(s_free[2], 1)

            def end_max(t):
                dve.tensor_reduce(part[:], acc4[:].rearrange("p j d -> p d j"), AX.X, ALU.max)
                dve.drain()
                dve.wait_ge(s_orowfree, t + 1)
                dve.tensor_tensor(stage2[:, bass.ds(t % 2, 1), :].rearrange("p a d -> p (a d)"), part[:],
                                  xs[:, bass.ds(t, 1), :].rearrange("p a c -> p (a c)"), ALU.add).then_inc(
                                      s_orow, 1)

            windows(dve, "dve2", add_max, start_max, end_max)


_INS = ["x", "adj", "L0_gnn_W", "L0_gnn_b", "L0_gnn_a_s", "L0_gnn_a_r", "L1_gnn_weight", "L1_gnn_bias"]


def kernel(**inputs):
    import numpy as np
    import concourse.bacc as bacc
    from concourse.bass_utils import run_bass_kernel_spmd

    nc = bacc.Bacc("TRN2", target_bir_lowering=False, num_devices=1)
    arrays, args = {}, []
    for name in _INS:
        a = np.ascontiguousarray(inputs[name])
        arrays[f"in_{name}"] = a
        args.append(nc.dram_tensor(f"in_{name}", a.shape, mybir.dt.from_np(a.dtype), kind="ExternalInput").ap())
    out = nc.dram_tensor("out_0", (N, D), F32, kind="ExternalOutput").ap()
    build(nc, *args, out)
    r = run_bass_kernel_spmd(nc, [arrays], core_ids=[0])
    return r.results[0]["out_0"]
```

```python
from contextlib import ExitStack

import concourse.bass as bass
from concourse import mybir

F32, BF16 = mybir.dt.float32, mybir.dt.bfloat16
I32, U32, U16 = mybir.dt.int32, mybir.dt.uint32, mybir.dt.uint16
ALU, ACT, AX = mybir.AluOpType, mybir.ActivationFunctionType, mybir.AxisListType

P = 128
N = 8192
D = 128
T = N // P
WORDS = 1024
PLANES = N // WORDS
BANK = 512
VSCALE = 512.0
GROUP = 4
WGROUPS = 8
WSLOTS = GROUP * WGROUPS
LIGHT = 48
LIGHT_STORE = 2 * WSLOTS
NARROW = 16
BATCH = 4
BPLANES = 4
PITCH = 132
ROWLEN = N
EPS = 1e-5
ALPHA = 0.2
MASKED = -9e15
UNUSED = -1e30
LOWEST = -3.4028234663852886e38


def build(nc, x, adj, W0, b0, a_s, a_r, W1, b1, out):
    ctx = ExitStack()
    with ctx:
        def sb(name, shape, dt=F32):
            return ctx.enter_context(nc.sbuf_tensor(name, shape, dt))

        def ps(name, shape, dt=F32):
            return ctx.enter_context(nc.psum_tensor(name, shape, dt))

        def sem(name):
            return ctx.enter_context(nc.semaphore(name))

        h_table = nc.dram_tensor("h_table", [N + 1, D + 1], F32).ap()
        p_table = nc.dram_tensor("p_table", [N + 1, D], F32).ap()
        packed = nc.dram_tensor("packed", [T, P, WORDS], U16).ap()
        lists = nc.dram_tensor("lists", [T, P, ROWLEN], U32).ap()

        xs = sb("xs", [P, T, D])
        a_buf = sb("a_buf", [P, 2, N])
        a_half = a_buf[:].bitcast(BF16).rearrange("p b (n two) -> p b n two", two=2)
        gathered = sb("gathered", [P, 2 * WSLOTS, PITCH])
        a_flat = a_buf[:].bitcast(BF16).rearrange("p b n -> p (b n)")
        y_part = [a_flat[:, i * N:(i + 1) * N] for i in range(3)]
        words_in = [a_flat[:, 3 * N + i * BATCH * WORDS:3 * N + (i + 1) * BATCH * WORDS].bitcast(U16).rearrange(
            "p (u n) -> p u n", u=BATCH) for i in range(2)]
        g_flat = gathered[:].bitcast(BF16).rearrange("p s c -> p (s c)")
        bit_rows = [g_flat[:, i * PLANES * BANK:(i + 1) * PLANES * BANK].rearrange("p (k n) -> p k n", k=PLANES)
                    for i in range(BPLANES)]
        slots_in = sb("slots_in", [P, 2, WSLOTS], U32)
        ident = sb("ident", [P, P])
        bit_ident = sb("bit_ident", [P, PLANES, P], BF16)
        ident_bf = sb("ident_bf", [P, P], BF16)
        ones_bf = sb("ones_bf", [P, P], BF16)
        word_no = sb("word_no", [P, WORDS], BF16)
        word_i = sb("word_i", [P, WORDS], I32)
        zeros_bf = sb("zeros_bf", [P, BANK], BF16)
        bit_mask = sb("bit_mask", [P, PLANES], I32)
        bit_node = sb("bit_node", [P, PLANES])
        chunk_base = sb("chunk_base", [P, PLANES])
        iota8 = sb("iota8", [P, PLANES], I32)
        ones_row = sb("ones_row", [P, P])
        w0_sb = sb("w0_sb", [P, D])
        w0_rhs = sb("w0_rhs", [P, D + 2])
        w0_aug = sb("w0_aug", [P, D + 2])
        b0_col = sb("b0_col", [P, 1])
        b0_rep = sb("b0_rep", [P, P])
        b0_aug = sb("b0_aug", [P, D + 2])
        w1_sb = sb("w1_sb", [P, D])
        b1_col = sb("b1_col", [P, 1])
        stats = sb("stats", [P, T, 6])
        mv = sb("mv", [P, T, 2])
        eps_col = sb("eps_col", [P, 1])
        rstd = sb("rstd", [P, T])
        hn = [sb(f"hn{i}", [P, BATCH, D]) for i in range(2)]
        hT = [sb(f"hT{i}", [P, BATCH, P]) for i in range(2)]
        stage = [sb(f"stage{i}", [P, BATCH, D + 1]) for i in range(2)]
        s_col = sb("s_col", [P, T])
        neutral = sb("neutral", [1, D + 1])
        deg4 = sb("deg4", [P, 4])
        deg_junk = sb("deg_junk", [P, N // 4], BF16)
        w_bf = sb("w_bf", [P, WORDS], BF16)
        wT = sb("wT", [P, WORDS], U16)
        meta_deg = sb("meta_deg", [1, T], I32)
        meta_groups = sb("meta_groups", [1, T], I32)
        chunk_rounds = sb("chunk_rounds", [1, PLANES], I32)
        mdeg = sb("mdeg", [1, 2])
        V = sb("V", [P, WORDS])
        words = sb("words", [P, LIGHT])
        words_i = sb("words_i", [P, LIGHT], I32)
        words_no = sb("words_no", [P, LIGHT], I32)
        bits = sb("bits", [P, LIGHT, PLANES], I32)
        node = sb("node", [P, LIGHT, PLANES])
        found = sb("found", [P, LIGHT_STORE])
        top8 = sb("top8", [P, 8])
        top8n = sb("top8n", [P, 8])
        cdeg = sb("cdeg", [P, 1])
        slots_out = sb("slots_out", [P, WORDS], U32)
        e_raw = sb("e_raw", [P, WSLOTS])
        e_sc = sb("e_sc", [P, WSLOTS])
        prob = sb("prob", [P, WSLOTS])
        m_old, m_win, m_neg, alpha, lsum, lwin, linv = (
            sb(n, [P, 1]) for n in ("m_old", "m_win", "m_neg", "alpha", "lsum", "lwin", "linv"))
        unused = sb("unused", [P, WSLOTS])
        acc = sb("acc", [P, D])
        part = sb("part", [P, D])
        acc4 = sb("acc4", [P, GROUP, D])
        stage2 = sb("stage2", [P, 2, D])
        outT = sb("outT", [P, BATCH, P])
        stage_p = sb("stage_p", [P, 2, BATCH * D])

        psV = ps("psV", [P, WORDS])
        psA = ps("psA", [P, BANK])
        psT = [ps(f"psT{i}", [P, BATCH, P]) for i in range(2)]
        psW = psT[0][:].rearrange("p u n -> p (u n)").bitcast(BF16)
        psH = [ps(f"psH{i}", [P, BANK]) for i in range(2)]
        psM = ps("psM", [P, BANK])

        s_held = sem("s_held")
        s_xin, s_w, s_b1 = sem("s_xin"), sem("s_w"), sem("s_b1")
        s_c0, s_c1, s_c2, s_const = sem("s_c0"), sem("s_c1"), sem("s_c2"), sem("s_const")
        s_waug = sem("s_waug")
        s_waug_sb = sem("s_waug_sb")
        s_var = [sem(f"s_var{l}") for l in range(2)]
        s_std = [sem(f"s_std{l}") for l in range(2)]
        s_hn = [sem(f"s_hn{l}") for l in range(2)]
        s_tr = [sem(f"s_tr{l}") for l in range(2)]
        s_hT = [sem(f"s_hT{l}") for l in range(2)]
        s_mm = [sem(f"s_mm{l}") for l in range(2)]
        s_row = [sem(f"s_row{l}") for l in range(2)]
        s_colsum, s_neutral = sem("s_colsum"), sem("s_neutral")
        s_tab = [sem(f"s_tab{i}") for i in range(2)]
        s_tabn = sem("s_tabn")
        s_table = sem("s_table")
        s_a = [sem("s_a0"), sem("s_a1")]
        s_deg, s_degT, s_meta, s_groups = sem("s_deg"), sem("s_degT"), sem("s_meta"), sem("s_groups")
        s_packed, s_wcopy, s_wtr, s_wt, s_wst = (sem(n) for n in ("s_packed", "s_wcopy", "s_wtr", "s_wt", "s_wst"))
        s_fill, s_drained, s_afree = sem("s_fill"), sem("s_drained"), sem("s_afree")
        s_cdeg, s_cT, s_cm = sem("s_cdeg"), sem("s_cT"), sem("s_cm")
        s_slots, s_stored = sem("s_slots"), sem("s_stored")
        s_load = [sem(f"s_load{f}") for f in range(2)]
        s_rows = [[sem(f"s_rows{f}{i}") for i in range(2)] for f in range(2)]
        s_free = [sem(f"s_free{f}") for f in range(2)]
        s_e, s_p, s_scaled, s_acc, s_accread, s_x1 = (
            sem("s_e"), sem("s_p"), sem("s_scaled"), sem("s_acc"), sem("s_accread"), sem("s_x1"))
        s_wordsin = [sem("s_wordsin0"), sem("s_wordsin1")]
        s_unpacked, s_bits, s_bitsfree = sem("s_unpacked"), sem("s_bits"), sem("s_bitsfree")
        s_sum, s_relu, s_ptr, s_prow, s_prowfree, s_pst = (
            sem(n) for n in ("s_sum", "s_relu", "s_ptr", "s_prow", "s_prowfree", "s_pst"))
        s_orow, s_orowfree, s_ost = sem("s_orow"), sem("s_orowfree"), sem("s_ost")

        def register(eng, name):
            r = eng.alloc_register(name)
            eng.reg_mov(r, 0)
            return r

        def bump(eng, r, n=1):
            eng.reg_add(r, r, n)

        def bounded(eng, value, least, most):
            r = eng.alloc_register(f"bounded{nc.next_id()}")
            eng.reg_mov(r, value)
            return eng.snap(r, min_val=least, max_val=most)

        def groups_here(eng, rest):
            left, most, r = (eng.alloc_register(f"here{nc.next_id()}") for _ in range(3))
            eng.reg_mov(left, rest)
            eng.reg_alu(most, left, WGROUPS, ALU.min)
            eng.reg_alu(r, most, 1, ALU.max)
            return eng.snap(r, min_val=1, max_val=WGROUPS)

        def tile(eng, t):
            return bounded(eng, t, 0, T - 1)

        def windows(eng, name, body, before=None, after=None, tiles=None):
            count = register(eng, f"{name}_k")
            with eng.Fori(0, T) as t:
                if before is not None:
                    before(t)
                groups = eng.value_load(meta_groups[0:1, bass.ds(t, 1)], min_val=1, max_val=ROWLEN // GROUP)
                with eng.Fori(0, (groups + (WGROUPS - 1)) // WGROUPS) as w:
                    body(t, w, eng.snap(count, min_val=0, max_val=1 << 17), groups - w * WGROUPS, groups)
                    bump(eng, count)
                if after is not None:
                    after(t)

        def slot_at(k, g):
            return (k % 2) * WSLOTS + g * GROUP

        def hold(eng, semaphore, value):
            eng.wait_ge(semaphore, value)
            eng.sem_inc(s_held, 1)

        def gathered_counts(eng, phase):
            return [register(eng, f"rows{phase}{b}_{nc.next_id()}") for b in range(2)]

        def wait_gathered(eng, phase, counts, n, groups):
            for b in range(2):
                with (eng.If(n % 2 == 1) if b == 0 else eng.Else()):
                    eng.reg_add(counts[b], counts[b], groups * (GROUP * 16))
                    hold(eng, s_rows[phase][b], eng.snap(counts[b], min_val=0, max_val=1 << 24))

        def load_window(eng, phase, t, w, k):
            eng.dma_start(slots_in[:, bass.ds(k % 2, 1), :].rearrange("p a n -> p (a n)"),
                          lists[bass.ds(t, 1), :, bass.ds(w * WSLOTS, WSLOTS)].rearrange(
                              "a p n -> (a p) n")).then_inc(s_load[phase], 16)

        block = ctx.enter_context(nc.Block())

        @block.sync
        def _(sp):
            sp.dma_start(xs[:, :, :], x.rearrange("(t p) c -> p t c", p=P)).then_inc(s_xin, 16)
            sp.dma_start(w0_sb[:], W0).then_inc(s_w, 16)
            sp.dma_start(w0_rhs[:, D:D + 1], a_s).then_inc(s_w, 16)
            sp.dma_start(w0_rhs[:, D + 1:D + 2], a_r).then_inc(s_w, 16)
            sp.dma_start(b0_col[:], b0.rearrange("(p a) -> p a", a=1)).then_inc(s_w, 16)
            sp.dma_start(w1_sb[:], W1).then_inc(s_w, 16)
            sp.dma_start(b1_col[:], b1.rearrange("(p a) -> p a", a=1)).then_inc(s_b1, 16)
            for u in range(2):
                sp.dma_start(a_buf[:, u, :], adj[u * P:(u + 1) * P, :]).then_inc(s_a[u], 16)

            with sp.Fori(0, T // BATCH // 2) as bp:
                for u in range(2):
                    b = 2 * bp + u
                    sp.wait_ge(s_row[0], b + 1)
                    sp.dma_start(h_table[bass.ds(b * (BATCH * P) + 1, BATCH * P), :].rearrange(
                        "(u p) c -> p u c", p=P), stage[u][:]).then_inc(s_tab[u], 16)
            for u in range(2):
                sp.wait_ge(s_tab[u], 16 * (T // BATCH // 2))
            sp.wait_ge(s_neutral, 3)
            sp.dma_start(h_table[0:1, :], neutral[0:1, :]).then_inc(s_tabn, 16)
            sp.wait_ge(s_tabn, 16)
            sp.sem_inc(s_table, 1)

            stores = register(sp, "sp_stores")
            offset = register(sp, "sp_offset")
            spare = register(sp, "sp_spare")

            def store_lists(t):
                hold(sp, s_meta, t + 1)
                deg = sp.value_load(meta_deg[0:1, bass.ds(t, 1)], min_val=1, max_val=N)
                with sp.If(deg <= LIGHT):
                    n = sp.snap(stores, min_val=0, max_val=1 << 12)
                    sp.wait_ge(s_slots, n + 1)
                    sp.dma_start(lists[bass.ds(t, 1), :, 0:LIGHT_STORE].rearrange("a p n -> (a p) n"),
                                 slots_out[:, 0:LIGHT_STORE]).then_inc(s_stored, 16)
                    bump(sp, stores)
                with sp.Else():
                    sp.reg_mov(offset, 0)
                    with sp.Fori(0, PLANES) as c:
                        n = sp.snap(stores, min_val=0, max_val=1 << 12)
                        sp.wait_ge(s_slots, n + 1)
                        at = sp.snap(offset, min_val=0, max_val=N - WORDS)
                        sp.dma_start(lists[bass.ds(t, 1), :, bass.ds(at, WORDS)].rearrange("a p n -> (a p) n"),
                                     slots_out[:, :]).then_inc(s_stored, 16)
                        sp.wait_ge(s_stored, (n + 1) * 16)
                        r = sp.value_load(chunk_rounds[0:1, bass.ds(c, 1)], min_val=0, max_val=WORDS // 8)
                        sp.reg_add(offset, offset, r * 8)
                        bump(sp, stores)
                n = sp.snap(stores, min_val=0, max_val=1 << 12)
                hold(sp, s_stored, n * 16)

            def load_adj(t, u):
                def load(t):
                    sp.wait_ge(s_afree, t - 1)
                    sp.dma_start(a_buf[:, u, :], adj[bass.ds(t * P, P), :]).then_inc(s_a[u], 16)

                if isinstance(t, int):
                    load(t)
                else:
                    with sp.If(t < T):
                        load(bounded(sp, t, 2, T - 1))
                        bump(sp, spare)

            deg_ahead = register(sp, "sp_deg_ahead")
            windows_seen = register(sp, "sp_windows")

            def load_first(t):
                k = sp.snap(windows_seen, min_val=0, max_val=1 << 17)
                hold(sp, s_free[0], k + 1)
                hold(sp, s_load[0], k * 16)
                load_window(sp, 0, t, 0, k)
                groups = sp.value_load(meta_groups[0:1, bass.ds(t, 1)], min_val=1, max_val=ROWLEN // GROUP)
                bump(sp, windows_seen, (groups + (WGROUPS - 1)) // WGROUPS)

            store_lists(0)
            sp.wait_ge(s_groups, 1)
            load_first(0)
            sp.wait_ge(s_deg, 1)
            load_adj(2, 0)
            with sp.Fori(0, T // 2) as tp:
                for u in range(2):
                    t = 2 * tp + u
                    with sp.If(t < T - 1):
                        ahead = tile(sp, t + 1)
                        hold(sp, s_meta, t + 2)
                        deg = sp.value_load(meta_deg[0:1, bass.ds(ahead, 1)], min_val=1, max_val=N)
                        sp.reg_mov(deg_ahead, deg)
                        with sp.If(deg <= LIGHT):
                            load_adj(ahead + 2, 1 - u)
                        store_lists(ahead)
                        with sp.If(sp.snap(deg_ahead, min_val=1, max_val=N) > LIGHT):
                            load_adj(ahead + 2, 1 - u)
                        hold(sp, s_groups, t + 2)
                        load_first(ahead)
                        bump(sp, spare)

            def load_words(c, u):
                sp.dma_start(words_in[u], packed[bass.ds(c * BATCH, BATCH), :, :].rearrange(
                    "u p n -> p u n")).then_inc(s_wordsin[u], 16)

            sp.wait_ge(s_wst, 16 * T)
            sp.wait_ge(s_var[1], 1)
            load_words(0, 0)
            load_words(1, 1)
            with sp.Fori(0, T // BATCH // 2) as cp:
                for u in range(2):
                    c = 2 * cp + u
                    with sp.If(c < T // BATCH - 2):
                        sp.wait_ge(s_unpacked, c + 1)
                        load_words(bounded(sp, c + 2, 0, T // BATCH - 1), u)
                    sp.wait_ge(s_prow, c + 1)
                    sp.dma_start(p_table[bass.ds(c * (BATCH * P) + 1, BATCH * P), :].rearrange(
                        "(u p) d -> p u d", p=P), stage_p[:, u, :].rearrange("p (u d) -> p u d", d=D)).then_inc(
                            s_pst, 16)
                    sp.wait_ge(s_pst, (c + 1) * 16)
                    sp.sem_inc(s_prowfree, 1)
            sp.wait_ge(s_neutral, 4)
            sp.dma_start(p_table[0:1, :], neutral[0:1, 0:D]).then_inc(s_tabn, 16)
            sp.wait_ge(s_tabn, 32)
            sp.sem_inc(s_table, 1)

            with sp.Fori(0, T) as t:
                sp.wait_ge(s_orow, t + 1)
                sp.dma_start(out[bass.ds(t * P, P), :],
                             stage2[:, bass.ds(t % 2, 1), :].rearrange("p a d -> p (a d)")).then_inc(s_ost, 16)
                sp.wait_ge(s_ost, (t + 1) * 16)
                sp.sem_inc(s_orowfree, 1)

        @block.gpsimd
        def _(pool):
            pool.memset(ident[:], 0.0).then_inc(s_c0, 1)
            pool.memset(w0_rhs[:, 0:D], 0.0).then_inc(s_c0, 1)
            pool.wait_ge(s_c0, 2)
            for m in (ident[:], w0_rhs[:, 0:D]):
                pool.affine_select(out=m, in_=m, compare_op=ALU.not_equal, fill=1.0, base=0,
                                   pattern=[[-1, P]], channel_multiplier=1).then_inc(s_c1, 1)
            pool.iota(word_i[:], pattern=[[1, WORDS]], base=0, channel_multiplier=0).then_inc(s_c1, 1)
            pool.iota(iota8[:], pattern=[[1, PLANES]], base=0, channel_multiplier=0).then_inc(s_c1, 1)
            pool.memset(ones_row[:], 1.0).then_inc(s_c1, 1)
            pool.memset(gathered[:], 0.0).then_inc(s_c2, 1)
            pool.wait_ge(s_c2, 1)
            pool.memset(gathered[:, :, D:D + 1], UNUSED).then_inc(s_c2, 1)
            pool.wait_ge(s_c2, 2)

            for phase, (table, width) in enumerate(((h_table, D + 1), (p_table, D))):
                pool.wait_ge(s_table, phase + 1)

                def before(t, phase=phase):
                    if phase == 0:
                        pool.wait_ge(s_groups, t + 1)

                def gather(t, w, k, rest, groups, phase=phase, table=table, width=width):
                    pool.wait_ge(s_load[phase], (k + 1) * 16)
                    pool.wait_ge(s_free[phase], k + 1)
                    for b in range(2):
                        def rows(g, b=b):
                            for j in range(g * GROUP, (g + 1) * GROUP):
                                pool.indirect_dma_start(
                                    gathered[:, b * WSLOTS + j, 0:width], None, table,
                                    bass.IndirectOffsetOnAxis(slots_in[:, b, j:j + 1], 0),
                                    bounds_check=N, oob_is_err=False).then_inc(s_rows[phase][b], 16)

                        with (pool.If(k % 2 == 0) if b == 0 else pool.Else()):
                            rows(0)
                            for g in range(1, WGROUPS):
                                with pool.If(rest > g):
                                    rows(g)

                windows(pool, f"pool{phase}", gather, before)

        @block.scalar
        def _(act):
            spare = register(act, "act_spare")

            def norm(layer):
                act.wait_ge(s_var[layer], 1)
                act.activation(rstd[:], mv[:, :, 1], ACT.Sqrt, bias=eps_col[:, 0:1]).then_inc(s_std[layer], 1)
                with act.Fori(0, T // BATCH // 2) as bp:
                    for u in range(2):
                        b = 2 * bp + u
                        act.wait_ge(s_tr[layer], b + 1)
                        act.activation(hT[u][:], psT[u][:], ACT.Relu).then_inc(s_hT[layer], 1)

            norm(0)

            def count_degrees(t, u):
                act.wait_ge(s_a[u], (t // 2 + 1) * 16)
                act.wait_ge(s_degT, t)
                for q in range(4):
                    if q:
                        act.drain()
                    last = act.activation(deg_junk[:], a_buf[:, u, q * (N // 4):(q + 1) * (N // 4)], ACT.Copy,
                                          accum_out=deg4[:, q:q + 1])
                last.then_inc(s_deg, 1)

            def keep_words(t):
                act.wait_ge(s_packed, t + 1)
                act.wait_ge(s_wtr, t)
                act.activation(w_bf[:], psV[:], ACT.Copy, scale=0.5).then_inc(s_wcopy, 1)
                act.wait_ge(s_wtr, t + 1)
                act.wait_ge(s_wst, 16 * t)
                act.activation(wT[:], psW, ACT.Copy).then_inc(s_wt, 1)
                act.wait_ge(s_wt, t + 1)
                act.dma_start(packed[bass.ds(t, 1), :, :].rearrange("a p n -> (a p) n"), wT[:]).then_inc(s_wst, 16)

            count_degrees(0, 0)
            count_degrees(1, 1)
            keep_words(0)
            keep_words(1)
            act.activation(alpha[:], lsum[:], ACT.Exp)
            count = register(act, "act_k")
            with act.Fori(0, T // 2) as tp:
                for u in range(2):
                    t = 2 * tp + u
                    act.wait_ge(s_groups, t + 1)
                    groups = act.value_load(meta_groups[0:1, bass.ds(t, 1)], min_val=1, max_val=ROWLEN // GROUP)
                    with act.If(t < T - 2):
                        ahead = tile(act, t + 2)
                        count_degrees(ahead, u)
                        keep_words(ahead)
                    with act.Fori(0, (groups + (WGROUPS - 1)) // WGROUPS) as w:
                        k = act.snap(count, min_val=0, max_val=1 << 17)
                        with act.If(groups > (w + 1) * WGROUPS):
                            act.wait_ge(s_free[0], k + 2)
                            act.wait_ge(s_load[0], (k + 1) * 16)
                            load_window(act, 0, t, bounded(act, w + 1, 1, N // WSLOTS - 1), k + 1)
                            bump(act, spare)
                        act.wait_ge(s_e, k + 1)
                        act.activation(prob[:], e_sc[:], ACT.Exp, bias=m_neg[:, 0:1], accum_out=lwin[:, 0:1])
                        act.activation(alpha[:], m_old[:], ACT.Exp, bias=m_neg[:, 0:1]).then_inc(s_p, 1)
                        bump(act, count)

            norm(1)
            act.wait_ge(s_b1, 16)
            with act.Fori(0, T // BATCH // 2) as cp:
                for u in range(2):
                    c = 2 * cp + u
                    act.wait_ge(s_sum, c + 1)
                    act.wait_ge(s_ptr, c)
                    act.activation(outT[:].rearrange("p u n -> p (u n)"), psA[:], ACT.Relu,
                                   bias=b1_col[:, 0:1], scale=0.5).then_inc(s_relu, 1)
                    act.wait_ge(s_ptr, c + 1)
                    act.wait_ge(s_prowfree, c + 1)
                    act.activation(stage_p[:, u, :], psT[1][:].rearrange("p u n -> p (u n)"),
                                   ACT.Copy).then_inc(s_prow, 1)

            act.dma_start(slots_in[:, 0, :], lists[0, :, 0:WSLOTS]).then_inc(s_load[1], 16)
            counts = gathered_counts(act, 1)
            last_groups = register(act, "act_last")

            def load_next(t, w, k, rest, groups):
                with act.If(k > 0):
                    wait_gathered(act, 1, counts, k, act.snap(last_groups, min_val=0, max_val=WGROUPS))
                    bump(act, spare)
                act.wait_ge(s_load[1], (k + 1) * 16)
                with act.If(rest > WGROUPS):
                    load_window(act, 1, t, bounded(act, w + 1, 1, N // WSLOTS - 1), k + 1)
                with act.Else():
                    with act.If(t < T - 1):
                        load_window(act, 1, tile(act, t + 1), 0, k + 1)
                    bump(act, spare)
                act.reg_mov(last_groups, groups_here(act, rest))

            windows(act, "act1", load_next)

        @block.tensor
        def _(pe):
            spare = register(pe, "pe_spare")
            pe.wait_ge(s_w, 80)
            pe.wait_ge(s_const, 1)
            pe.matmul(psH[0][:, 0:D + 2], w0_sb[:], w0_rhs[:], start=True, stop=True)
            pe.matmul(psH[1][:, 0:D + 2], b0_rep[:], w0_rhs[:], start=True, stop=True).then_inc(s_waug, 1)
            pe.wait_ge(s_waug_sb, 1)

            def norm(layer, weights):
                def transposes(b, u):
                    pe.wait_ge(s_hn[layer], b + 1)
                    for j in range(BATCH):
                        last = pe.transpose(psT[u][:, j, :], hn[u][:, j, :], ident[:])
                    last.then_inc(s_tr[layer], 1)

                transposes(0, 0)
                with pe.Fori(0, T // BATCH // 2) as bp:
                    for u in range(2):
                        b = 2 * bp + u
                        pe.wait_ge(s_hT[layer], b + 1)
                        pe.wait_ge(s_row[layer], b)
                        for j in range(BATCH):
                            last = pe.matmul(psH[u][:, j * D:(j + 1) * D], hT[u][:, j, :], weights[:, 0:D],
                                             start=True, stop=True)
                            if layer == 0:
                                last = pe.matmul(psV[:, u * BANK + 2 * j:u * BANK + 2 * j + 2], hT[u][:, j, :],
                                                 weights[:, D:D + 2], start=True, stop=True)
                        last.then_inc(s_mm[layer], 1)
                        with pe.If(b < T // BATCH - 1):
                            transposes(bounded(pe, b + 1, 1, T // BATCH - 1), 1 - u)

            norm(0, w0_aug[:])
            pe.wait_ge(s_colsum, 1)
            pe.matmul(psM[0:1, :], ones_row[:, 0:1], acc4[:].rearrange("p j d -> p (j d)"),
                      start=True, stop=True).then_inc(s_colsum, 1)
            pe.wait_ge(s_neutral, 3)

            fills = register(pe, "pe_fills")
            heavy_chunks = register(pe, "pe_chunks")

            def fill_wait():
                n = pe.snap(fills, min_val=0, max_val=1 << 12)
                pe.wait_ge(s_drained, n)
                bump(pe, fills)

            def number_words():
                for h in range(2):
                    last = pe.matmul(psV[:, h * BANK:(h + 1) * BANK], ones_bf[:],
                                     word_no[:, h * BANK:(h + 1) * BANK], start=False, stop=True,
                                     skip_group_check=True)
                return last

            def degrees(t):
                pe.wait_ge(s_deg, t + 1)
                pe.wait_ge(s_meta, t)
                for q in range(4):
                    last = pe.matmul(psM[0:1, 0:P], deg4[:, q:q + 1], ident[:], start=(q == 0), stop=(q == 3))
                last.then_inc(s_degT, 1)

            def load_degree(t):
                pe.wait_ge(s_meta, t + 1)
                return pe.value_load(meta_deg[0:1, bass.ds(t, 1)], min_val=1, max_val=N)

            deg_ahead = register(pe, "pe_deg_ahead")

            def pack(t, u):
                fill_wait()
                pe.wait_ge(s_a[u], (t // 2 + 1) * 16)
                for h in range(2):
                    for k in range(PLANES):
                        at = k * WORDS + h * BANK
                        last = pe.matmul(psV[:, h * BANK:(h + 1) * BANK], bit_ident[:, k, :],
                                         a_half[:, u, at:at + BANK, 1], start=(k == 0), stop=(k == PLANES - 1))
                last.then_inc(s_packed, 1)
                pe.wait_ge(s_wcopy, t + 1)
                number_words().then_inc(s_fill, 1)
                pe.wait_ge(s_wt, t)
                for b in range(WORDS // P):
                    last = pe.transpose(psW[:, b * P:(b + 1) * P], w_bf[:, b * P:(b + 1) * P], ident_bf[:])
                last.then_inc(s_wtr, 1)
                pe.reg_mov(deg_ahead, load_degree(t))
                with pe.If(pe.snap(deg_ahead, min_val=0, max_val=N) <= LIGHT):
                    pe.drain().then_inc(s_afree, 1)

            def pack_heavy(t, u):
                with pe.If(pe.snap(deg_ahead, min_val=0, max_val=N) > LIGHT):
                    with pe.Fori(0, PLANES) as c:
                        fill_wait()
                        for h in range(2):
                            pe.matmul(psV[:, h * BANK:(h + 1) * BANK], bit_ident[:, 0, :],
                                      a_half[:, u, bass.ds(c * WORDS + h * BANK, BANK), 1],
                                      start=True, stop=True)
                        number_words().then_inc(s_fill, 1)
                        bump(pe, heavy_chunks)
                        n = pe.snap(heavy_chunks, min_val=0, max_val=1 << 12)
                        pe.wait_ge(s_cdeg, n)
                        pe.matmul(psH[1][0:1, 0:P], cdeg[:], ident[:], start=True, stop=True).then_inc(s_cT, 1)
                        bump(pe, spare)
                    pe.drain().then_inc(s_afree, 1)
                    bump(pe, spare)

            degrees(0)
            pack(0, 0)
            pack_heavy(0, 0)
            degrees(1)
            pack(1, 1)

            def add_groups(n, k):
                with pe.Fori(0, n) as g:
                    pe.matmul(psA[:].rearrange("p (j d) -> p j d", d=D), ident[:],
                              gathered[:, bass.ds(slot_at(k, g), GROUP), 0:D],
                              start=False, stop=False)

            count = register(pe, "pe_k")
            with pe.Fori(0, T // 2) as tp:
                for u in range(2):
                    t = 2 * tp + u
                    with pe.If(t < T - 1):
                        pack_heavy(tile(pe, t + 1), 1 - u)
                        bump(pe, spare)
                    with pe.If(t < T - 2):
                        ahead = tile(pe, t + 2)
                        degrees(ahead)
                        pack(ahead, u)
                        bump(pe, spare)
                    pe.wait_ge(s_groups, t + 1)
                    groups = pe.value_load(meta_groups[0:1, bass.ds(t, 1)], min_val=1, max_val=ROWLEN // GROUP)
                    with pe.Fori(0, (groups + (WGROUPS - 1)) // WGROUPS) as w:
                        k = pe.snap(count, min_val=0, max_val=1 << 17)
                        pe.wait_ge(s_accread, k)
                        pe.matmul(psA[:], ones_bf[:], zeros_bf[:], start=True, stop=False)
                        pe.wait_ge(s_scaled, k + 1)
                        add_groups(groups_here(pe, groups - w * WGROUPS), k)
                        pe.matmul(psA[:], ones_bf[:], zeros_bf[:], start=False, stop=True).then_inc(s_acc, 1)
                        pe.drain().then_inc(s_free[0], 1)
                        bump(pe, count)

            norm(1, w1_sb[:])

            with pe.Fori(0, T // BATCH) as c:
                for b in range(WORDS // P):
                    pe.wait_ge(s_bits, c * (WORDS // P) + (b + 1))
                    if b == 0:
                        pe.wait_ge(s_relu, c)
                        pe.wait_ge(s_row[1], T // BATCH)
                    for k in range(PLANES):
                        at = (k * (WORDS // P) + b) * D
                        for i in range(3):
                            last = pe.matmul(psA[:], y_part[i][:, at:at + D], bit_rows[b % BPLANES][:, k, :],
                                             start=(b == 0 and k == 0 and i == 0),
                                             stop=(b == WORDS // P - 1 and k == PLANES - 1 and i == 2))
                    last.then_inc(s_bitsfree, 1)
                pe.drain().then_inc(s_sum, 1)
                pe.wait_ge(s_relu, c + 1)
                pe.wait_ge(s_prow, c)
                for j in range(BATCH):
                    last = pe.transpose(psT[1][:, j, :], outT[:, j, :], ident[:])
                last.then_inc(s_ptr, 1)

        @block.vector
        def _(dve):
            spare = register(dve, "dve_spare")
            dve.memset(eps_col[:], EPS)
            dve.memset(ones_bf[:], 1.0)
            dve.memset(zeros_bf[:], 0.0)
            dve.memset(unused[:], UNUSED)
            dve.memset(lsum[:], 0.0)
            dve.memset(acc[:], 0.0)
            for f in range(2):
                dve.sem_inc(s_free[f], 2)
            dve.sem_inc(s_prowfree, 2)
            dve.sem_inc(s_bitsfree, BPLANES)
            dve.sem_inc(s_orowfree, 2)
            dve.wait_ge(s_c1, 5)
            dve.tensor_copy(ident_bf[:], ident[:])
            for k in range(PLANES):
                dve.tensor_scalar(bit_ident[:, k, :], ident[:], float(2 ** (k + 1)), None, ALU.mult)
                dve.memset(bit_mask[:, k:k + 1], WORDS << k)
            dve.tensor_scalar(bit_node[:], iota8[:], float(WORDS), 1.0, ALU.mult, ALU.add)
            dve.tensor_scalar(chunk_base[:], iota8[:], float(WORDS), float(1 - WORDS), ALU.mult, ALU.add)
            hi, lo = bits[:].rearrange("p a b -> p (a b)"), node[:].rearrange("p a b -> p (a b)")
            for at in range(0, WORDS, LIGHT * PLANES):
                n = min(LIGHT * PLANES, WORDS - at)
                dve.drain()
                dve.tensor_scalar(hi[:, 0:n], word_i[:, at:at + n], WORDS - 8, None, ALU.bitwise_and)
                dve.drain()
                dve.tensor_scalar(V[:, at:at + n], hi[:, 0:n], 1.0 / VSCALE, None, ALU.mult)
                dve.drain()
                dve.tensor_scalar(hi[:, 0:n], word_i[:, at:at + n], 7, None, ALU.bitwise_and)
                dve.tensor_scalar(V[:, at:at + n], V[:, at:at + n], ident[:, 0:1], None, ALU.mult)
                dve.drain()
                dve.tensor_scalar(lo[:, 0:n], hi[:, 0:n], 1.0 / VSCALE, None, ALU.mult)
                dve.drain()
                dve.scalar_tensor_tensor(word_no[:, at:at + n], lo[:, 0:n], ident[:, 1:2], V[:, at:at + n],
                                         ALU.mult, ALU.add)
            dve.wait_ge(s_w, 80)
            dve.tensor_scalar(b0_rep[:], ones_row[:], b0_col[:, 0:1], None, ALU.mult)
            dve.drain().then_inc(s_const, 1)
            dve.wait_ge(s_waug, 1)
            dve.tensor_copy(w0_aug[:], psH[0][:, 0:D + 2])
            dve.tensor_copy(b0_aug[:], psH[1][:, 0:D + 2])
            dve.drain().then_inc(s_waug_sb, 1)

            def norm(layer):
                with dve.Fori(0, T) as t:
                    dve.bn_stats(stats[:, bass.ds(t, 1), :].rearrange("p a c -> p (a c)"),
                                 xs[:, bass.ds(t, 1), :].rearrange("p a c -> p (a c)"))
                dve.drain()
                for t in range(T):
                    dve.bn_aggr(mv[:, t, :], stats[:, t, :])
                dve.drain().then_inc(s_var[layer], 1)
                dve.wait_ge(s_std[layer], 1)
                dve.reciprocal(rstd[:], rstd[:])
                dve.drain()

                def normalize(b, u):
                    for j in range(BATCH):
                        t = b * BATCH + j
                        last = dve.tensor_scalar(hn[u][:, j, :], xs[:, bass.ds(t, 1), :].rearrange("p a c -> p (a c)"),
                                                 mv[:, bass.ds(t, 1), 0], rstd[:, bass.ds(t, 1)],
                                                 ALU.subtract, ALU.mult)
                    last.then_inc(s_hn[layer], 1)

                def plus(to, product, bias):
                    dve.tensor_tensor(to, product, bias, ALU.add)

                normalize(0, 0)
                with dve.Fori(0, T // BATCH // 2) as bp:
                    for u in range(2):
                        b = 2 * bp + u
                        with dve.If(b < T // BATCH - 1):
                            normalize(bounded(dve, b + 1, 1, T // BATCH - 1), 1 - u)
                        dve.wait_ge(s_mm[layer], b + 1)
                        product = psH[u][:].rearrange("p (j d) -> p j d", d=D)
                        rows = stage[u][:, :, 0:D]
                        if layer == 0:
                            dve.wait_ge(s_tab[u], bp * 16)
                            sr = psV[:, u * BANK:u * BANK + 2 * BATCH].rearrange("p (j c) -> p j c", c=2)
                            plus(rows, product, b0_aug[:, 0:D].unsqueeze(1).to_broadcast([P, BATCH, D]))
                            plus(stage[u][:, :, D], sr[:, :, 1], b0_aug[:, D + 1:D + 2].to_broadcast([P, BATCH]))
                            plus(s_col[:, bass.ds(b * BATCH, BATCH)], sr[:, :, 0],
                                 b0_aug[:, D:D + 1].to_broadcast([P, BATCH]))
                            dve.drain().then_inc(s_row[layer], 1)
                            plus(acc4[:], acc4[:], rows)
                        else:
                            hi, mid, lo = (y_part[i][:, bass.ds(b * (BATCH * D), BATCH * D)].rearrange(
                                "p (j d) -> p j d", d=D) for i in range(3))
                            dve.tensor_copy(hi, product)
                            dve.drain()
                            dve.tensor_tensor(rows, product, hi, ALU.subtract)
                            dve.drain()
                            dve.tensor_copy(mid, rows)
                            dve.drain()
                            dve.tensor_tensor(lo, rows, mid, ALU.subtract)
                            dve.drain().then_inc(s_row[layer], 1)

            dve.memset(acc4[:], 0.0)
            dve.wait_ge(s_xin, 16)
            norm(0)
            dve.drain().then_inc(s_colsum, 1)
            dve.wait_ge(s_colsum, 2)
            dve.tensor_reduce(part[0:1, :], psM[0:1, :].rearrange("p (j d) -> p d j", d=D), AX.X, ALU.add)
            dve.drain()
            dve.tensor_scalar(neutral[0:1, 0:D], part[0:1, :], 1.0 / N, None, ALU.mult)
            dve.memset(neutral[0:1, D:D + 1], MASKED)
            dve.drain().then_inc(s_neutral, 3)

            fills = register(dve, "dve_fills")
            stores = register(dve, "dve_stores")
            chunks = register(dve, "dve_chunks")

            groups_now = register(dve, "dve_groups_now")
            groups_next = register(dve, "dve_groups_next")

            deg_next = register(dve, "dve_deg_next")

            def load_degree(t):
                hold(dve, s_meta, t + 1)
                dve.reg_mov(deg_next, dve.value_load(meta_deg[0:1, bass.ds(t, 1)], min_val=1, max_val=N))

            def meta(t):
                dve.wait_ge(s_degT, t + 1)
                dve.reduce_max(mdeg[0:1, 0:1], psM[0:1, 0:P], axis=AX.X)
                dve.drain()
                dve.tensor_scalar(meta_deg[0:1, bass.ds(t, 1)], mdeg[0:1, 0:1], 1.0, None, ALU.max)
                dve.tensor_scalar(meta_groups[0:1, bass.ds(t, 1)], mdeg[0:1, 0:1],
                                  1.0, float(GROUP - 1), ALU.max, ALU.add)
                dve.drain()
                dve.tensor_scalar(meta_groups[0:1, bass.ds(t, 1)], meta_groups[0:1, bass.ds(t, 1)],
                                  2, None, ALU.logical_shift_right)
                dve.drain().then_inc(s_meta, 1)

            def wait_fill():
                n = dve.snap(fills, min_val=0, max_val=1 << 12)
                dve.wait_ge(s_fill, n + 1)
                bump(dve, fills)

            def wait_stored():
                n = dve.snap(stores, min_val=0, max_val=1 << 12)
                dve.wait_ge(s_stored, n * 16)
                bump(dve, stores)

            def expand(n, deg):
                dve.tensor_scalar(words_i[:, 0:n], words[:, 0:n], VSCALE, None, ALU.mult)
                dve.drain()
                dve.tensor_scalar(words_no[:, 0:n], words_i[:, 0:n], WORDS - 1, None, ALU.bitwise_and)
                dve.tensor_tensor(bits[:, 0:n, :], words_i[:, 0:n].unsqueeze(2).to_broadcast([P, n, PLANES]),
                                  bit_mask[:].unsqueeze(1).to_broadcast([P, n, PLANES]), ALU.bitwise_and)
                dve.drain()
                dve.tensor_tensor(node[:, 0:n, :], words_no[:, 0:n].unsqueeze(2).to_broadcast([P, n, PLANES]),
                                  bit_node[:].unsqueeze(1).to_broadcast([P, n, PLANES]), ALU.add)
                dve.drain()
                flat = node[:, 0:n, :].rearrange("p a b -> p (a b)")
                dve.scalar_tensor_tensor(flat, bits[:, 0:n, :].rearrange("p a b -> p (a b)"), 0.0, flat,
                                         ALU.is_gt, ALU.mult)
                dve.drain()
                dve.max(found[:, 0:8], flat)
                for r in range(8, n, 8):
                    with dve.If(deg > r):
                        dve.drain()
                        dve.match_replace(flat, found[:, r - 8:r], flat, 0.0)
                        dve.drain()
                        dve.max(found[:, r:r + 8], flat)
                dve.drain()

            def extract_light(deg):
                dve.memset(words[:], 0.0)
                dve.memset(found[:], 0.0)
                wait_fill()
                dve.drain()
                dve.max(words[:, 0:8], psV[:])
                dve.drain()
                with dve.If(deg > 8):
                    dve.match_replace(V[:], words[:, 0:8], psV[:], 0.0).then_inc(s_drained, 1)
                    dve.drain()
                    dve.max(words[:, 8:16], V[:])
                with dve.Else():
                    dve.sem_inc(s_drained, 1)
                for r in range(16, LIGHT, 8):
                    with dve.If(deg > r):
                        dve.drain()
                        dve.match_replace(V[:], words[:, r - 8:r], V[:], 0.0)
                        dve.drain()
                        dve.max(words[:, r:r + 8], V[:])
                dve.drain()
                with dve.If(deg > NARROW):
                    expand(LIGHT, deg)
                    bump(dve, spare)
                with dve.Else():
                    expand(NARROW, deg)
                    bump(dve, spare)
                wait_stored()
                dve.tensor_copy(slots_out[:, 0:LIGHT_STORE], found[:])
                dve.drain().then_inc(s_slots, 1)

            def extract_heavy(t):
                groups = meta_groups[0:1, bass.ds(t, 1)]
                dve.memset(mdeg[0:1, 1:2], 0.0)
                wait_fill()
                dve.sem_inc(s_drained, 1)
                with dve.Fori(0, PLANES) as c:
                    wait_fill()
                    dve.drain()
                    dve.tensor_scalar(V[:], psV[:], 2.0, 0.0, ALU.is_ge, ALU.add, accum_out=cdeg[:, 0:1])
                    dve.drain().then_inc(s_cdeg, 1)
                    dve.tensor_copy(V[:], psV[:]).then_inc(s_drained, 1)
                    wait_stored()
                    dve.memset(slots_out[:], 0)
                    bump(dve, chunks)
                    n = dve.snap(chunks, min_val=0, max_val=1 << 12)
                    dve.wait_ge(s_cT, n)
                    dve.reduce_max(mdeg[0:1, 0:1], psH[1][0:1, 0:P], axis=AX.X)
                    dve.drain()
                    rounds = chunk_rounds[0:1, bass.ds(c, 1)]
                    dve.tensor_scalar(rounds, mdeg[0:1, 0:1], 7.0, None, ALU.add)
                    dve.drain()
                    dve.tensor_scalar(rounds, rounds, 3, None, ALU.logical_shift_right)
                    dve.drain()
                    dve.scalar_tensor_tensor(mdeg[0:1, 1:2], rounds, 2.0, mdeg[0:1, 1:2], ALU.mult, ALU.add)
                    dve.drain().then_inc(s_cm, 1)
                    hold(dve, s_cm, n)
                    todo = dve.value_load(rounds, min_val=0, max_val=WORDS // 8)
                    with dve.If(todo > 0):
                        with dve.Fori(0, todo) as r:
                            dve.max(top8[:], V[:])
                            dve.drain()
                            dve.match_replace(V[:], top8[:], V[:], 0.0)
                            dve.tensor_scalar(top8n[:], top8[:], VSCALE, chunk_base[:, bass.ds(c, 1)],
                                              ALU.mult, ALU.add)
                            dve.drain()
                            dve.scalar_tensor_tensor(slots_out[:, bass.ds(r * 8, 8)], top8[:], 2.0, top8n[:],
                                                     ALU.is_ge, ALU.mult)
                            dve.drain()
                        bump(dve, spare)
                    dve.drain().then_inc(s_slots, 1)
                dve.tensor_scalar(groups, mdeg[0:1, 1:2], 1.0, None, ALU.max)
                dve.drain()

            def extract(t):
                deg = dve.snap(deg_next, min_val=1, max_val=N)
                with dve.If(deg <= LIGHT):
                    extract_light(deg)
                    dve.reg_mov(groups_next, (deg + (GROUP - 1)) // GROUP)
                with dve.Else():
                    extract_heavy(t)
                    dve.reg_mov(groups_next, dve.value_load(meta_groups[0:1, bass.ds(t, 1)], min_val=1,
                                                            max_val=ROWLEN // GROUP))
                dve.drain().then_inc(s_groups, 1)

            count = register(dve, "dve_k")

            rows_seen = gathered_counts(dve, 0)

            def add_up(k):
                dve.wait_ge(s_acc, k)
                dve.tensor_reduce(part[:], psA[:].rearrange("p (j d) -> p d j", d=D), AX.X, ALU.add).then_inc(
                    s_accread, 1)
                dve.drain()
                dve.scalar_tensor_tensor(acc[:], acc[:], alpha[:, 0:1], part[:], ALU.mult, ALU.add)
                dve.drain()

            def close_tile(t):
                dve.reciprocal(linv[:], lsum[:])
                dve.drain()
                row = xs[:, bass.ds(t, 1), :].rearrange("p a c -> p (a c)")
                dve.scalar_tensor_tensor(row, acc[:], linv[:, 0:1], row, ALU.mult, ALU.add)

            def weigh(k, first, n):
                rows = gathered[:, bass.ds((k % 2) * WSLOTS + first, n), 0:D]
                dve.tensor_tensor(rows, rows, prob[:, first:first + n].unsqueeze(2).to_broadcast([P, n, D]), ALU.mult)

            def attend_window(t, k, rest):
                n = groups_here(dve, rest)
                r_col = gathered[:, bass.ds((k % 2) * WSLOTS, WSLOTS), D]
                wait_gathered(dve, 0, rows_seen, k + 1, n)
                dve.tensor_scalar(e_raw[:], r_col, s_col[:, bass.ds(t, 1)], None, ALU.add)
                dve.drain()
                dve.scalar_tensor_tensor(e_sc[:], e_raw[:], ALPHA, e_raw[:], ALU.mult, ALU.max)
                dve.tensor_copy(r_col, unused[:])
                dve.drain()
                dve.reduce_max(m_win[:], e_sc[:], axis=AX.X)
                dve.drain()
                dve.tensor_scalar(m_neg[:], m_win[:], m_old[:, 0:1], -1.0, ALU.max, ALU.mult)
                dve.drain().then_inc(s_e, 1)
                dve.wait_ge(s_p, k + 1)
                weigh(k, 0, 2 * GROUP)
                with dve.If(n > 2):
                    weigh(k, 2 * GROUP, 2 * GROUP)
                with dve.If(n > 4):
                    weigh(k, 4 * GROUP, 4 * GROUP)
                dve.tensor_scalar(m_old[:], m_neg[:], -1.0, None, ALU.mult)
                dve.scalar_tensor_tensor(lsum[:], lsum[:], alpha[:, 0:1], lwin[:], ALU.mult, ALU.add)
                dve.drain().then_inc(s_scaled, 1)

            meta(0)
            load_degree(0)
            extract(0)
            meta(1)
            load_degree(1)
            with dve.Fori(0, T) as t:
                dve.reg_mov(groups_now, dve.snap(groups_next, min_val=1, max_val=ROWLEN // GROUP))
                with dve.If(t < T - 1):
                    extract(tile(dve, t + 1))
                    bump(dve, spare)
                with dve.If(t < T - 2):
                    meta(tile(dve, t + 2))
                    bump(dve, spare)
                with dve.If(t > 0):
                    add_up(dve.snap(count, min_val=0, max_val=1 << 17))
                    close_tile(bounded(dve, t - 1, 0, T - 2))
                    bump(dve, spare)
                dve.memset(m_old[:], LOWEST)
                groups = dve.snap(groups_now, min_val=1, max_val=ROWLEN // GROUP)
                with dve.Fori(0, (groups + (WGROUPS - 1)) // WGROUPS) as w:
                    k = dve.snap(count, min_val=0, max_val=1 << 17)
                    with dve.If(w > 0):
                        add_up(k)
                        bump(dve, spare)
                    attend_window(t, k, groups - w * WGROUPS)
                    bump(dve, count)
                with dve.If(t < T - 2):
                    load_degree(tile(dve, t + 2))
                    bump(dve, spare)
            add_up(dve.snap(count, min_val=0, max_val=1 << 17))
            close_tile(T - 1)
            dve.drain()

            norm(1)

            with dve.Fori(0, T // BATCH // 2) as cp:
                for u in range(2):
                    c = 2 * cp + u
                    dve.wait_ge(s_wordsin[u], (cp + 1) * 16)
                    for b in range(WORDS // P):
                        dve.wait_ge(s_bitsfree, c * (WORDS // P) + (b + 1))
                        for k in range(PLANES):
                            last = dve.tensor_scalar(
                                bit_rows[b % BPLANES][:, k, :].bitcast(U16).rearrange("p (u n) -> p u n", n=P),
                                words_in[u][:, :, b * P:(b + 1) * P], 14 - k, 1 << 14,
                                ALU.logical_shift_left, ALU.bitwise_and)
                        last.then_inc(s_bits, 1)
                    dve.drain().then_inc(s_unpacked, 1)
            dve.memset(neutral[0:1, :], LOWEST)
            dve.drain().then_inc(s_neutral, 1)
            rows_max = gathered_counts(dve, 1)

            def start_max(t):
                dve.memset(acc4[:], LOWEST)
                dve.drain()

            def add_max(t, w, k, rest, groups):
                n = groups_here(dve, rest)
                wait_gathered(dve, 1, rows_max, k + 1, n)
                with dve.Fori(0, n) as g:
                    dve.tensor_tensor(acc4[:], acc4[:], gathered[:, bass.ds(slot_at(k, g), GROUP), 0:D], ALU.max)
                    dve.drain()
                dve.drain().then_inc(s_free[1], 1)

            def end_max(t):
                dve.tensor_reduce(part[:], acc4[:].rearrange("p j d -> p d j"), AX.X, ALU.max)
                dve.drain()
                dve.wait_ge(s_orowfree, t + 1)
                dve.tensor_tensor(stage2[:, bass.ds(t % 2, 1), :].rearrange("p a d -> p (a d)"), part[:],
                                  xs[:, bass.ds(t, 1), :].rearrange("p a c -> p (a c)"), ALU.add).then_inc(
                                      s_orow, 1)

            windows(dve, "dve2", add_max, start_max, end_max)


_INS = ["x", "adj", "L0_gnn_W", "L0_gnn_b", "L0_gnn_a_s", "L0_gnn_a_r", "L1_gnn_weight", "L1_gnn_bias"]


def kernel(**inputs):
    import numpy as np
    import concourse.bacc as bacc
    from concourse.bass_utils import run_bass_kernel_spmd

    nc = bacc.Bacc("TRN2", target_bir_lowering=False, num_devices=1)
    arrays, args = {}, []
    for name in _INS:
        a = np.ascontiguousarray(inputs[name])
        arrays[f"in_{name}"] = a
        args.append(nc.dram_tensor(f"in_{name}", a.shape, mybir.dt.from_np(a.dtype), kind="ExternalInput").ap())
    out = nc.dram_tensor("out_0", (N, D), F32, kind="ExternalOutput").ap()
    build(nc, *args, out)
    r = run_bass_kernel_spmd(nc, [arrays], core_ids=[0])
    return r.results[0]["out_0"]
```

```python
from contextlib import ExitStack

import concourse.bass as bass
from concourse import mybir

F32, BF16 = mybir.dt.float32, mybir.dt.bfloat16
I32, U32, U16 = mybir.dt.int32, mybir.dt.uint32, mybir.dt.uint16
ALU, ACT, AX = mybir.AluOpType, mybir.ActivationFunctionType, mybir.AxisListType

P = 128
N = 8192
D = 128
T = N // P
WORDS = 1024
PLANES = N // WORDS
BANK = 512
VSCALE = 512.0
GROUP = 4
WGROUPS = 8
WSLOTS = GROUP * WGROUPS
LIGHT = 48
LIGHT_STORE = 2 * WSLOTS
NARROW = 16
MIDDLE = 24
BATCH = 4
BPLANES = 4
PITCH = 132
ROWLEN = N
ROWWINDOWS = ROWLEN // WSLOTS
CLASSES = 16
EPS = 1e-5
ALPHA = 0.2
MASKED = -9e15
UNUSED = -1e30
LOWEST = -3.4028234663852886e38


def build(nc, x, adj, W0, b0, a_s, a_r, W1, b1, out):
    ctx = ExitStack()
    with ctx:
        def sb(name, shape, dt=F32):
            return ctx.enter_context(nc.sbuf_tensor(name, shape, dt))

        def ps(name, shape, dt=F32):
            return ctx.enter_context(nc.psum_tensor(name, shape, dt))

        def sem(name):
            return ctx.enter_context(nc.semaphore(name))

        h_table = nc.dram_tensor("h_table", [N + 1, D + 1], F32).ap()
        p_table = nc.dram_tensor("p_table", [N + 1, D], F32).ap()
        packed = nc.dram_tensor("packed", [T, P, WORDS], U16).ap()
        lists = nc.dram_tensor("lists", [T, P, ROWLEN], U32).ap()
        list_windows = lists.rearrange("t p (w n) -> (t p w) n", n=WSLOTS)
        order = nc.dram_tensor("order", [N, 2], I32).ap()
        order_max = nc.dram_tensor("order_max", [T, 1], I32).ap()

        xs = sb("xs", [P, T, D])
        a_buf = sb("a_buf", [P, 2, N])
        a_half = a_buf[:].bitcast(BF16).rearrange("p b (n two) -> p b n two", two=2)
        gathered = sb("gathered", [P, 2 * WSLOTS, PITCH])
        a_flat = a_buf[:].bitcast(BF16).rearrange("p b n -> p (b n)")
        y_part = [a_flat[:, i * N:(i + 1) * N] for i in range(3)]
        words_in = [a_flat[:, 3 * N + i * BATCH * WORDS:3 * N + (i + 1) * BATCH * WORDS].bitcast(U16).rearrange(
            "p (u n) -> p u n", u=BATCH) for i in range(2)]
        g_flat = gathered[:].bitcast(BF16).rearrange("p s c -> p (s c)")
        bit_rows = [g_flat[:, i * PLANES * BANK:(i + 1) * PLANES * BANK].rearrange("p (k n) -> p k n", k=PLANES)
                    for i in range(BPLANES)]
        slots_in = sb("slots_in", [P, 2, WSLOTS], U32)
        ident = sb("ident", [P, P])
        bit_ident = sb("bit_ident", [P, PLANES, P], BF16)
        ident_bf = sb("ident_bf", [P, P], BF16)
        ones_bf = sb("ones_bf", [P, P], BF16)
        word_no = sb("word_no", [P, WORDS], BF16)
        word_i = sb("word_i", [P, WORDS], I32)
        zeros_bf = sb("zeros_bf", [P, BANK], BF16)
        bit_mask = sb("bit_mask", [P, PLANES], I32)
        bit_node = sb("bit_node", [P, PLANES])
        chunk_base = sb("chunk_base", [P, PLANES])
        iota8 = sb("iota8", [P, PLANES], I32)
        ones_row = sb("ones_row", [P, P])
        w0_sb = sb("w0_sb", [P, D])
        w0_rhs = sb("w0_rhs", [P, D + 2])
        w0_aug = sb("w0_aug", [P, D + 2])
        b0_col = sb("b0_col", [P, 1])
        b0_rep = sb("b0_rep", [P, P])
        b0_aug = sb("b0_aug", [P, D + 2])
        w1_sb = sb("w1_sb", [P, D])
        b1_col = sb("b1_col", [P, 1])
        stats = sb("stats", [P, T, 6])
        mv = sb("mv", [P, T, 2])
        eps_col = sb("eps_col", [P, 1])
        rstd = sb("rstd", [P, T])
        hn = [sb(f"hn{i}", [P, BATCH, D]) for i in range(2)]
        hT = [sb(f"hT{i}", [P, BATCH, P]) for i in range(2)]
        stage = [sb(f"stage{i}", [P, BATCH, D + 1]) for i in range(2)]
        s_col = sb("s_col", [P, T])
        neutral = sb("neutral", [1, D + 1])
        degree = sb("degree", [P, 1])
        deg_junk = sb("deg_junk", [P, BANK], BF16)
        w_bf = sb("w_bf", [P, WORDS], BF16)
        wT = sb("wT", [P, WORDS], U16)
        meta_deg = sb("meta_deg", [1, T], I32)
        meta_groups = sb("meta_groups", [1, T], I32)
        chunk_rounds = sb("chunk_rounds", [1, PLANES], I32)
        mdeg = sb("mdeg", [1, 2])
        V = sb("V", [P, WORDS])
        words = sb("words", [P, LIGHT])
        words_i = sb("words_i", [P, LIGHT], I32)
        words_no = sb("words_no", [P, LIGHT], I32)
        bits = sb("bits", [P, LIGHT, PLANES], I32)
        node = sb("node", [P, LIGHT, PLANES])
        found = sb("found", [P, LIGHT_STORE])
        top8 = sb("top8", [P, 8])
        top8n = sb("top8n", [P, 8])
        cdeg = sb("cdeg", [P, 1])
        slots_out = sb("slots_out", [P, WORDS], U32)
        row_degree = sb("row_degree", [P, T])
        row_no = sb("row_no", [P, T], I32)
        row_groups = sb("row_groups", [P, T], I32)
        tile_groups = sb("tile_groups", [P, T])
        groups_f = sb("groups_f", [1, T])
        row_class = sb("row_class", [P, T])
        class_i = sb("class_i", [P, CLASSES], I32)
        class_no = sb("class_no", [P, CLASSES])
        one_hot = w_bf[:].rearrange("p (c t) -> p c t", t=T)
        rank_f = sb("rank_f", [P, T])
        rank = sb("rank", [P, T], U32)
        ranked = sb("ranked", [P, T, 2], I32)
        sorted_rows = sb("sorted_rows", [P, T, 2], U32)
        sorted_t = sb("sorted_t", [T, P, 2], I32)
        sorted_max = sb("sorted_max", [T, 1], I32)
        sorted_groups = sb("sorted_groups", [1, T], I32)
        upper = sb("upper", [P, P])
        upper_bf = sb("upper_bf", [P, P], BF16)
        first_lists = sb("first_lists", [P, T, WSLOTS], U32)
        more_list = sb("more_list", [P, WSLOTS], U32)
        more_index = sb("more_index", [P, 1], U32)
        window_no, groups_left, past_end = (sb(n, [P, 1]) for n in ("window_no", "groups_left", "past_end"))
        out_row = sb("out_row", [P, 2], U32)
        zeros_u = sb("zeros_u", [P, WSLOTS], U32)
        e_raw = sb("e_raw", [P, WSLOTS])
        e_sc = sb("e_sc", [P, WSLOTS])
        prob = sb("prob", [P, WSLOTS])
        m_old, m_win, m_neg, alpha, lsum, lwin, linv = (
            sb(n, [P, 1]) for n in ("m_old", "m_win", "m_neg", "alpha", "lsum", "lwin", "linv"))
        unused = sb("unused", [P, WSLOTS])
        acc = sb("acc", [P, D])
        part = sb("part", [P, D])
        acc4 = sb("acc4", [P, GROUP, D])
        stage2 = sb("stage2", [P, 2, D])
        outT = sb("outT", [P, BATCH, P])
        stage_p = sb("stage_p", [P, 2, BATCH * D])

        psV = ps("psV", [P, WORDS])
        psA = ps("psA", [P, BANK])
        psT = [ps(f"psT{i}", [P, BATCH, P]) for i in range(2)]
        psW = psT[0][:].rearrange("p u n -> p (u n)").bitcast(BF16)
        psH = [ps(f"psH{i}", [P, BANK]) for i in range(2)]
        psM = ps("psM", [P, BANK])

        s_held = sem("s_held")
        s_xin, s_w, s_b1 = sem("s_xin"), sem("s_w"), sem("s_b1")
        s_c0, s_c1, s_c2, s_const = sem("s_c0"), sem("s_c1"), sem("s_c2"), sem("s_const")
        s_waug = sem("s_waug")
        s_waug_sb = sem("s_waug_sb")
        s_var = [sem(f"s_var{l}") for l in range(2)]
        s_std = [sem(f"s_std{l}") for l in range(2)]
        s_hn = [sem(f"s_hn{l}") for l in range(2)]
        s_tr = [sem(f"s_tr{l}") for l in range(2)]
        s_hT = [sem(f"s_hT{l}") for l in range(2)]
        s_mm = [sem(f"s_mm{l}") for l in range(2)]
        s_row = [sem(f"s_row{l}") for l in range(2)]
        s_colsum, s_neutral = sem("s_colsum"), sem("s_neutral")
        s_tab = [sem(f"s_tab{i}") for i in range(2)]
        s_tabn = sem("s_tabn")
        s_table = sem("s_table")
        s_a = [sem("s_a0"), sem("s_a1")]
        s_slabs, s_deg, s_degT, s_meta, s_groups = sem("s_slabs"), sem("s_deg"), sem("s_degT"), sem("s_meta"), sem("s_groups")
        s_packed, s_wcopy, s_wtr, s_wt, s_wst = (sem(n) for n in ("s_packed", "s_wcopy", "s_wtr", "s_wt", "s_wst"))
        s_fill, s_drained, s_afree = sem("s_fill"), sem("s_drained"), sem("s_afree")
        s_cdeg, s_cT, s_cm = sem("s_cdeg"), sem("s_cT"), sem("s_cm")
        s_slots, s_stored = sem("s_slots"), sem("s_stored")
        s_load = [sem(f"s_load{f}") for f in range(2)]
        s_rows = [[sem(f"s_rows{f}{i}") for i in range(2)] for f in range(2)]
        s_free = [sem(f"s_free{f}") for f in range(2)]
        s_e, s_p, s_scaled, s_acc, s_accread, s_x1 = (
            sem("s_e"), sem("s_p"), sem("s_scaled"), sem("s_acc"), sem("s_accread"), sem("s_x1"))
        s_wordsin = [sem("s_wordsin0"), sem("s_wordsin1")]
        s_unpacked, s_bits, s_bitsfree = sem("s_unpacked"), sem("s_bits"), sem("s_bitsfree")
        s_sum, s_relu, s_ptr, s_prow, s_prowfree, s_pst = (
            sem(n) for n in ("s_sum", "s_relu", "s_ptr", "s_prow", "s_prowfree", "s_pst"))
        s_spread_in, s_spread, s_onehot, s_counted, s_ranked = (
            sem(n) for n in ("s_spread_in", "s_spread", "s_onehot", "s_counted", "s_ranked"))
        s_order, s_sorted, s_sorted_t, s_lists = (sem(n) for n in ("s_order", "s_sorted", "s_sorted_t", "s_lists"))
        s_max, s_maxst, s_maxin = sem("s_max"), sem("s_maxst"), sem("s_maxin")
        s_index, s_more, s_slotted = sem("s_index"), sem("s_more"), sem("s_slotted")
        s_orow, s_xout = sem("s_orow"), sem("s_xout")
        s_added = [sem("s_added0"), sem("s_added1")]

        def register(eng, name):
            r = eng.alloc_register(name)
            eng.reg_mov(r, 0)
            return r

        def bump(eng, r, n=1):
            eng.reg_add(r, r, n)

        def bounded(eng, value, least, most):
            r = eng.alloc_register(f"bounded{nc.next_id()}")
            eng.reg_mov(r, value)
            return eng.snap(r, min_val=least, max_val=most)

        def groups_here(eng, rest):
            left, most, r = (eng.alloc_register(f"here{nc.next_id()}") for _ in range(3))
            eng.reg_mov(left, rest)
            eng.reg_alu(most, left, WGROUPS, ALU.min)
            eng.reg_alu(r, most, 1, ALU.max)
            return eng.snap(r, min_val=1, max_val=WGROUPS)

        def tile(eng, t):
            return bounded(eng, t, 0, T - 1)

        def windows(eng, name, body, before=None, after=None, counts=meta_groups):
            count = register(eng, f"{name}_k")
            with eng.Fori(0, T) as t:
                if before is not None:
                    before(t)
                groups = eng.value_load(counts[0:1, bass.ds(t, 1)], min_val=1, max_val=ROWLEN // GROUP)
                with eng.Fori(0, (groups + (WGROUPS - 1)) // WGROUPS) as w:
                    body(t, w, eng.snap(count, min_val=0, max_val=1 << 17), groups - w * WGROUPS, groups)
                    bump(eng, count)
                if after is not None:
                    after(t)

        def slot_at(k, g):
            return (k % 2) * WSLOTS + g * GROUP

        def hold(eng, semaphore, value):
            eng.wait_ge(semaphore, value)
            eng.sem_inc(s_held, 1)

        def gathered_counts(eng, phase):
            return [register(eng, f"rows{phase}{b}_{nc.next_id()}") for b in range(2)]

        def wait_gathered(eng, phase, counts, n, groups):
            for b in range(2):
                with (eng.If(n % 2 == 1) if b == 0 else eng.Else()):
                    eng.reg_add(counts[b], counts[b], groups * (GROUP * 16))
                    hold(eng, s_rows[phase][b], eng.snap(counts[b], min_val=0, max_val=1 << 24))

        def load_window(eng, phase, t, w, k):
            eng.dma_start(slots_in[:, bass.ds(k % 2, 1), :].rearrange("p a n -> p (a n)"),
                          lists[bass.ds(t, 1), :, bass.ds(w * WSLOTS, WSLOTS)].rearrange(
                              "a p n -> (a p) n")).then_inc(s_load[phase], 16)

        block = ctx.enter_context(nc.Block())

        @block.sync
        def _(sp):
            sp.dma_start(xs[:, :, :], x.rearrange("(t p) c -> p t c", p=P)).then_inc(s_xin, 16)
            sp.dma_start(w0_sb[:], W0).then_inc(s_w, 16)
            sp.dma_start(w0_rhs[:, D:D + 1], a_s).then_inc(s_w, 16)
            sp.dma_start(w0_rhs[:, D + 1:D + 2], a_r).then_inc(s_w, 16)
            sp.dma_start(b0_col[:], b0.rearrange("(p a) -> p a", a=1)).then_inc(s_w, 16)
            sp.dma_start(w1_sb[:], W1).then_inc(s_w, 16)
            sp.dma_start(b1_col[:], b1.rearrange("(p a) -> p a", a=1)).then_inc(s_b1, 16)
            for u in range(2):
                sp.dma_start(a_buf[:, u, :], adj[u * P:(u + 1) * P, :]).then_inc(s_a[u], 16)

            with sp.Fori(0, T // BATCH // 2) as bp:
                for u in range(2):
                    b = 2 * bp + u
                    sp.wait_ge(s_row[0], b + 1)
                    sp.dma_start(h_table[bass.ds(b * (BATCH * P) + 1, BATCH * P), :].rearrange(
                        "(u p) c -> p u c", p=P), stage[u][:]).then_inc(s_tab[u], 16)
            for u in range(2):
                sp.wait_ge(s_tab[u], 16 * (T // BATCH // 2))
            sp.wait_ge(s_neutral, 3)
            sp.dma_start(h_table[0:1, :], neutral[0:1, :]).then_inc(s_tabn, 16)
            sp.wait_ge(s_tabn, 16)
            sp.sem_inc(s_table, 1)

            stores = register(sp, "sp_stores")
            offset = register(sp, "sp_offset")
            spare = register(sp, "sp_spare")

            def store_lists(t):
                hold(sp, s_meta, t + 1)
                deg = sp.value_load(meta_deg[0:1, bass.ds(t, 1)], min_val=1, max_val=N)
                with sp.If(deg <= LIGHT):
                    n = sp.snap(stores, min_val=0, max_val=1 << 12)
                    sp.wait_ge(s_slots, n + 1)
                    sp.dma_start(lists[bass.ds(t, 1), :, 0:LIGHT_STORE].rearrange("a p n -> (a p) n"),
                                 slots_out[:, 0:LIGHT_STORE]).then_inc(s_stored, 16)
                    bump(sp, stores)
                with sp.Else():
                    sp.reg_mov(offset, 0)
                    with sp.Fori(0, PLANES) as c:
                        n = sp.snap(stores, min_val=0, max_val=1 << 12)
                        sp.wait_ge(s_slots, n + 1)
                        at = sp.snap(offset, min_val=0, max_val=N - WORDS)
                        sp.dma_start(lists[bass.ds(t, 1), :, bass.ds(at, WORDS)].rearrange("a p n -> (a p) n"),
                                     slots_out[:, :]).then_inc(s_stored, 16)
                        sp.wait_ge(s_stored, (n + 1) * 16)
                        r = sp.value_load(chunk_rounds[0:1, bass.ds(c, 1)], min_val=0, max_val=WORDS // 8)
                        sp.reg_add(offset, offset, r * 8)
                        bump(sp, stores)
                n = sp.snap(stores, min_val=0, max_val=1 << 12)
                hold(sp, s_stored, n * 16)

            def load_adj(t, u):
                def load(t):
                    sp.wait_ge(s_afree, t - 1)
                    sp.dma_start(a_buf[:, u, :], adj[bass.ds(t * P, P), :]).then_inc(s_a[u], 16)

                if isinstance(t, int):
                    load(t)
                else:
                    with sp.If(t < T):
                        load(bounded(sp, t, 2, T - 1))
                        bump(sp, spare)

            windows_seen = register(sp, "sp_windows")

            def load_first(t):
                k = sp.snap(windows_seen, min_val=0, max_val=1 << 17)
                hold(sp, s_free[0], k + 1)
                hold(sp, s_load[0], k * 16)
                load_window(sp, 0, t, 0, k)
                groups = sp.value_load(meta_groups[0:1, bass.ds(t, 1)], min_val=1, max_val=ROWLEN // GROUP)
                bump(sp, windows_seen, (groups + (WGROUPS - 1)) // WGROUPS)

            store_lists(0)
            sp.wait_ge(s_groups, 1)
            load_first(0)
            sp.wait_ge(s_deg, 1)
            load_adj(2, 0)
            with sp.Fori(0, T // 2) as tp:
                for u in range(2):
                    t = 2 * tp + u
                    with sp.If(t < T - 1):
                        ahead = tile(sp, t + 1)
                        store_lists(ahead)
                        hold(sp, s_groups, t + 2)
                        load_first(ahead)
                        load_adj(ahead + 2, 1 - u)
                        bump(sp, spare)

            def load_words(c, u):
                sp.dma_start(words_in[u], packed[bass.ds(c * BATCH, BATCH), :, :].rearrange(
                    "u p n -> p u n")).then_inc(s_wordsin[u], 16)

            sp.wait_ge(s_wst, 16 * T)
            sp.wait_ge(s_var[1], 1)
            load_words(0, 0)
            load_words(1, 1)
            sp.dma_start(out.rearrange("(t p) c -> p t c", p=P), xs[:, :, :]).then_inc(s_xout, 16)
            with sp.Fori(0, T // BATCH // 2) as cp:
                for u in range(2):
                    c = 2 * cp + u
                    with sp.If(c < T // BATCH - 2):
                        sp.wait_ge(s_unpacked, c + 1)
                        load_words(bounded(sp, c + 2, 0, T // BATCH - 1), u)
                    sp.wait_ge(s_prow, c + 1)
                    sp.dma_start(p_table[bass.ds(c * (BATCH * P) + 1, BATCH * P), :].rearrange(
                        "(u p) d -> p u d", p=P), stage_p[:, u, :].rearrange("p (u d) -> p u d", d=D)).then_inc(
                            s_pst, 16)
                    sp.wait_ge(s_pst, (c + 1) * 16)
                    sp.sem_inc(s_prowfree, 1)
            sp.wait_ge(s_neutral, 4)
            sp.dma_start(p_table[0:1, :], neutral[0:1, 0:D]).then_inc(s_tabn, 16)
            sp.wait_ge(s_tabn, 32)
            sp.sem_inc(s_table, 1)

            sp.wait_ge(s_xout, 16)
            for b in range(2):
                sp.wait_ge(s_added[b], 16 * (T // 2))

        @block.gpsimd
        def _(pool):
            pool.memset(ident[:], 0.0).then_inc(s_c0, 1)
            pool.memset(w0_rhs[:, 0:D], 0.0).then_inc(s_c0, 1)
            pool.wait_ge(s_c0, 2)
            for m in (ident[:], w0_rhs[:, 0:D]):
                pool.affine_select(out=m, in_=m, compare_op=ALU.not_equal, fill=1.0, base=0,
                                   pattern=[[-1, P]], channel_multiplier=1).then_inc(s_c1, 1)
            pool.iota(word_i[:], pattern=[[1, WORDS]], base=0, channel_multiplier=0).then_inc(s_c1, 1)
            pool.iota(iota8[:], pattern=[[1, PLANES]], base=0, channel_multiplier=0).then_inc(s_c1, 1)
            pool.memset(ones_row[:], 1.0).then_inc(s_c1, 1)
            pool.iota(class_i[:], pattern=[[-1, CLASSES]], base=CLASSES - 1, channel_multiplier=0).then_inc(s_c1, 1)
            pool.iota(row_no[:], pattern=[[P, T]], base=0, channel_multiplier=1).then_inc(s_c1, 1)
            pool.memset(upper[:], 1.0).then_inc(s_c2, 1)
            pool.memset(gathered[:], 0.0).then_inc(s_c2, 1)
            pool.wait_ge(s_c2, 2)
            pool.affine_select(out=upper[:], in_=upper[:], compare_op=ALU.is_gt, fill=0.0, base=0,
                               pattern=[[1, P]], channel_multiplier=-1).then_inc(s_c1, 1)
            pool.memset(gathered[:, :, D:D + 1], UNUSED).then_inc(s_c2, 1)
            pool.wait_ge(s_c2, 3)

            def gather_rows(phase, b, g, table, width):
                for j in range(g * GROUP, (g + 1) * GROUP):
                    pool.indirect_dma_start(
                        gathered[:, b * WSLOTS + j, 0:width], None, table,
                        bass.IndirectOffsetOnAxis(slots_in[:, b, j:j + 1], 0),
                        bounds_check=N, oob_is_err=False).then_inc(s_rows[phase][b], 16)

            pool.wait_ge(s_table, 1)

            def groups_known(t):
                pool.wait_ge(s_groups, t + 1)

            def gather_h(t, w, k, rest, groups):
                pool.wait_ge(s_load[0], (k + 1) * 16)
                pool.wait_ge(s_free[0], k + 1)
                for b in range(2):
                    with (pool.If(k % 2 == 0) if b == 0 else pool.Else()):
                        gather_rows(0, b, 0, h_table, D + 1)
                        for g in range(1, WGROUPS):
                            with pool.If(rest > g):
                                gather_rows(0, b, g, h_table, D + 1)

            windows(pool, "pool0", gather_h, groups_known)

            pool.wait_ge(s_ranked, 1)
            for t in range(T):
                pool.indirect_dma_start(order, bass.IndirectOffsetOnAxis(rank[:, t:t + 1], 0), ranked[:, t, :],
                                        None, bounds_check=N - 1).then_inc(s_order, 16)
            pool.wait_ge(s_order, 16 * T)
            pool.dma_start(sorted_t[:], order.rearrange("(t p) c -> t p c", p=P).bitcast(I32)).then_inc(s_sorted_t, 16)
            pool.dma_start(sorted_rows[:], order.rearrange("(t p) c -> p t c", p=P).bitcast(U32)).then_inc(s_sorted, 16)
            pool.wait_ge(s_sorted, 16)
            for t in range(T):
                pool.indirect_dma_start(first_lists[:, t, :], None, list_windows,
                                        bass.IndirectOffsetOnAxis(sorted_rows[:, t, 0:1], 0),
                                        bounds_check=N * ROWWINDOWS - 1, oob_is_err=False).then_inc(s_lists, 16)
            pool.wait_ge(s_max, 1)
            pool.dma_start(order_max, sorted_max[:]).then_inc(s_maxst, 16)
            pool.wait_ge(s_maxst, 16)
            pool.dma_start(sorted_groups[:], order_max.rearrange("t a -> a t")).then_inc(s_maxin, 16)

            pool.wait_ge(s_table, 2)
            pool.wait_ge(s_xout, 16)
            hold(pool, s_maxin, 16)
            lists_more = register(pool, "pool_more")

            def gather_p(t, w, k, rest, groups):
                pool.wait_ge(s_slotted, k + 1)
                for b in range(2):
                    with (pool.If(k % 2 == 0) if b == 0 else pool.Else()):
                        gather_rows(1, b, 0, p_table, D)
                        for g in range(1, WGROUPS):
                            with pool.If(rest > g):
                                if g == WGROUPS - 1:
                                    with pool.If(rest > WGROUPS):
                                        bump(pool, lists_more)
                                        hold(pool, s_index, pool.snap(lists_more, min_val=0, max_val=1 << 17))
                                        pool.indirect_dma_start(
                                            more_list[:], None, list_windows,
                                            bass.IndirectOffsetOnAxis(more_index[:], 0),
                                            bounds_check=N * ROWWINDOWS - 1, oob_is_err=False).then_inc(s_more, 16)
                                gather_rows(1, b, g, p_table, D)

            def add_out(b):
                pool.indirect_dma_start(out, bass.IndirectOffsetOnAxis(out_row[:, b:b + 1], 0), stage2[:, b, :],
                                        None, bounds_check=N - 1, compute_op=ALU.add).then_inc(s_added[b], 16)

            def add_last(t):
                with pool.If(t > 0):
                    hold(pool, s_orow, t)
                    with pool.If(t % 2 == 1):
                        add_out(0)
                    with pool.Else():
                        add_out(1)

            windows(pool, "pool1", gather_p, after=add_last, counts=sorted_groups)
            pool.wait_ge(s_orow, T)
            add_out((T - 1) % 2)

        @block.scalar
        def _(act):
            spare = register(act, "act_spare")

            def norm(layer):
                act.wait_ge(s_var[layer], 1)
                act.activation(rstd[:], mv[:, :, 1], ACT.Sqrt, bias=eps_col[:, 0:1]).then_inc(s_std[layer], 1)
                with act.Fori(0, T // BATCH // 2) as bp:
                    for u in range(2):
                        b = 2 * bp + u
                        act.wait_ge(s_tr[layer], b + 1)
                        act.activation(hT[u][:], psT[u][:], ACT.Relu).then_inc(s_hT[layer], 1)

            norm(0)

            def count_degrees(t):
                act.wait_ge(s_slabs, t + 1)
                act.wait_ge(s_meta, t)
                act.activation(deg_junk[:], psT[1][:].rearrange("p u n -> p (u n)"), ACT.Copy,
                               accum_out=degree[:, 0:1]).then_inc(s_deg, 1)

            def copy_words(t):
                act.wait_ge(s_packed, t + 1)
                act.wait_ge(s_wtr, t)
                act.activation(w_bf[:], psV[:], ACT.Copy, scale=0.5).then_inc(s_wcopy, 1)
                count_degrees(t)

            def keep_words(t):
                act.wait_ge(s_wtr, t + 1)
                act.wait_ge(s_wst, 16 * t)
                act.activation(wT[:], psW, ACT.Copy).then_inc(s_wt, 1)
                act.wait_ge(s_wt, t + 1)
                act.dma_start(packed[bass.ds(t, 1), :, :].rearrange("a p n -> (a p) n"), wT[:]).then_inc(s_wst, 16)

            for t in range(2):
                copy_words(t)
                keep_words(t)
            act.activation(alpha[:], lsum[:], ACT.Exp)
            act.drain()
            count = register(act, "act_k")
            with act.Fori(0, T // 2) as tp:
                for u in range(2):
                    t = 2 * tp + u
                    act.wait_ge(s_groups, t + 1)
                    groups = act.value_load(meta_groups[0:1, bass.ds(t, 1)], min_val=1, max_val=ROWLEN // GROUP)
                    with act.If(t < T - 2):
                        copy_words(tile(act, t + 2))
                        bump(act, spare)
                    with act.Fori(0, (groups + (WGROUPS - 1)) // WGROUPS) as w:
                        k = act.snap(count, min_val=0, max_val=1 << 17)
                        with act.If(groups > (w + 1) * WGROUPS):
                            act.wait_ge(s_free[0], k + 2)
                            act.wait_ge(s_load[0], (k + 1) * 16)
                            load_window(act, 0, t, bounded(act, w + 1, 1, N // WSLOTS - 1), k + 1)
                            bump(act, spare)
                        act.wait_ge(s_e, k + 1)
                        act.activation(prob[:], e_sc[:], ACT.Exp, bias=m_neg[:, 0:1], accum_out=lwin[:, 0:1])
                        act.activation(alpha[:], m_old[:], ACT.Exp, bias=m_neg[:, 0:1]).then_inc(s_p, 1)
                        bump(act, count)
                    with act.If(t < T - 2):
                        keep_words(tile(act, t + 2))
                        bump(act, spare)

            norm(1)
            act.wait_ge(s_b1, 16)
            with act.Fori(0, T // BATCH // 2) as cp:
                for u in range(2):
                    c = 2 * cp + u
                    act.wait_ge(s_sum, c + 1)
                    act.wait_ge(s_ptr, c)
                    act.activation(outT[:].rearrange("p u n -> p (u n)"), psA[:], ACT.Relu,
                                   bias=b1_col[:, 0:1], scale=0.5).then_inc(s_relu, 1)
                    act.wait_ge(s_ptr, c + 1)
                    act.wait_ge(s_prowfree, c + 1)
                    act.activation(stage_p[:, u, :], psT[1][:].rearrange("p u n -> p (u n)"),
                                   ACT.Copy).then_inc(s_prow, 1)

            act.wait_ge(s_lists, 16 * T)
            hold(act, s_maxin, 16)
            lists_more = register(act, "act_more")

            def place_slots(t, w, k, rest, groups):
                hold(act, s_free[1], k + 1)
                slots = slots_in[:, bass.ds(k % 2, 1), :].rearrange("p a n -> p (a n)")
                with act.If(w == 0):
                    act.activation(slots, first_lists[:, bass.ds(t, 1), :].rearrange("p a n -> p (a n)"), ACT.Copy)
                with act.Else():
                    bump(act, lists_more, 16)
                    hold(act, s_more, act.snap(lists_more, min_val=0, max_val=1 << 21))
                    act.activation(slots, more_list[:], ACT.Copy)
                    act.drain()
                    act.activation(more_list[:], zeros_u[:], ACT.Copy)
                act.drain().then_inc(s_slotted, 1)

            windows(act, "act1", place_slots, counts=sorted_groups)

        @block.tensor
        def _(pe):
            spare = register(pe, "pe_spare")
            pe.wait_ge(s_w, 80)
            pe.wait_ge(s_const, 1)
            pe.matmul(psH[0][:, 0:D + 2], w0_sb[:], w0_rhs[:], start=True, stop=True)
            pe.matmul(psH[1][:, 0:D + 2], b0_rep[:], w0_rhs[:], start=True, stop=True).then_inc(s_waug, 1)
            pe.wait_ge(s_waug_sb, 1)

            def norm(layer, weights):
                def transposes(b, u):
                    pe.wait_ge(s_hn[layer], b + 1)
                    for j in range(BATCH):
                        last = pe.transpose(psT[u][:, j, :], hn[u][:, j, :], ident[:])
                    last.then_inc(s_tr[layer], 1)

                transposes(0, 0)
                with pe.Fori(0, T // BATCH // 2) as bp:
                    for u in range(2):
                        b = 2 * bp + u
                        pe.wait_ge(s_hT[layer], b + 1)
                        pe.wait_ge(s_row[layer], b)
                        for j in range(BATCH):
                            last = pe.matmul(psH[u][:, j * D:(j + 1) * D], hT[u][:, j, :], weights[:, 0:D],
                                             start=True, stop=True)
                            if layer == 0:
                                last = pe.matmul(psV[:, u * BANK + 2 * j:u * BANK + 2 * j + 2], hT[u][:, j, :],
                                                 weights[:, D:D + 2], start=True, stop=True)
                        last.then_inc(s_mm[layer], 1)
                        with pe.If(b < T // BATCH - 1):
                            transposes(bounded(pe, b + 1, 1, T // BATCH - 1), 1 - u)

            norm(0, w0_aug[:])
            pe.wait_ge(s_colsum, 1)
            pe.matmul(psM[0:1, :], ones_row[:, 0:1], acc4[:].rearrange("p j d -> p (j d)"),
                      start=True, stop=True).then_inc(s_colsum, 1)
            pe.wait_ge(s_neutral, 3)

            fills = register(pe, "pe_fills")
            heavy_chunks = register(pe, "pe_chunks")

            def fill_wait():
                n = pe.snap(fills, min_val=0, max_val=1 << 12)
                pe.wait_ge(s_drained, n)
                bump(pe, fills)

            def number_words():
                for h in range(2):
                    last = pe.matmul(psV[:, h * BANK:(h + 1) * BANK], ones_bf[:],
                                     word_no[:, h * BANK:(h + 1) * BANK], start=False, stop=True,
                                     skip_group_check=True)
                return last

            def degrees(t):
                pe.wait_ge(s_deg, t + 1)
                pe.wait_ge(s_meta, t)
                pe.matmul(psM[0:1, 0:P], degree[:], ident[:], start=True, stop=True).then_inc(s_degT, 1)

            def load_degree(t):
                pe.wait_ge(s_meta, t + 1)
                return pe.value_load(meta_deg[0:1, bass.ds(t, 1)], min_val=1, max_val=N)

            deg_ahead = register(pe, "pe_deg_ahead")

            def pack(t, u):
                fill_wait()
                pe.wait_ge(s_a[u], (t // 2 + 1) * 16)
                for h in range(2):
                    for k in range(PLANES):
                        at = k * WORDS + h * BANK
                        last = pe.matmul(psV[:, h * BANK:(h + 1) * BANK], bit_ident[:, k, :],
                                         a_half[:, u, at:at + BANK, 1], start=(k == 0), stop=(k == PLANES - 1))
                last.then_inc(s_packed, 1)
                pe.wait_ge(s_deg, t)
                slabs = N // BANK
                for q in range(slabs):
                    last = pe.matmul(psT[1][:].rearrange("p u n -> p (u n)"), ident_bf[:],
                                     a_half[:, u, q * BANK:(q + 1) * BANK, 1], start=(q == 0), stop=(q == slabs - 1))
                last.then_inc(s_slabs, 1)
                pe.wait_ge(s_wcopy, t + 1)
                number_words().then_inc(s_fill, 1)
                pe.wait_ge(s_wt, t)
                for b in range(WORDS // P):
                    last = pe.transpose(psW[:, b * P:(b + 1) * P], w_bf[:, b * P:(b + 1) * P], ident_bf[:])
                last.then_inc(s_wtr, 1)
                degrees(t)

            def pack_heavy(t, u):
                pe.reg_mov(deg_ahead, load_degree(t))
                with pe.If(pe.snap(deg_ahead, min_val=0, max_val=N) <= LIGHT):
                    pe.drain().then_inc(s_afree, 1)
                with pe.If(pe.snap(deg_ahead, min_val=0, max_val=N) > LIGHT):
                    with pe.Fori(0, PLANES) as c:
                        fill_wait()
                        for h in range(2):
                            pe.matmul(psV[:, h * BANK:(h + 1) * BANK], bit_ident[:, 0, :],
                                      a_half[:, u, bass.ds(c * WORDS + h * BANK, BANK), 1],
                                      start=True, stop=True)
                        number_words().then_inc(s_fill, 1)
                        bump(pe, heavy_chunks)
                        n = pe.snap(heavy_chunks, min_val=0, max_val=1 << 12)
                        pe.wait_ge(s_cdeg, n)
                        pe.matmul(psH[1][0:1, 0:P], cdeg[:], ident[:], start=True, stop=True).then_inc(s_cT, 1)
                        bump(pe, spare)
                    pe.drain().then_inc(s_afree, 1)
                    bump(pe, spare)

            pack(0, 0)
            pack_heavy(0, 0)
            pack(1, 1)

            def add_groups(n, k):
                with pe.Fori(0, n) as g:
                    pe.matmul(psA[:].rearrange("p (j d) -> p j d", d=D), ident[:],
                              gathered[:, bass.ds(slot_at(k, g), GROUP), 0:D],
                              start=False, stop=False)

            count = register(pe, "pe_k")
            with pe.Fori(0, T // 2) as tp:
                for u in range(2):
                    t = 2 * tp + u
                    with pe.If(t < T - 1):
                        pack_heavy(tile(pe, t + 1), 1 - u)
                        bump(pe, spare)
                    with pe.If(t < T - 2):
                        ahead = tile(pe, t + 2)
                        pack(ahead, u)
                        bump(pe, spare)
                    pe.wait_ge(s_groups, t + 1)
                    groups = pe.value_load(meta_groups[0:1, bass.ds(t, 1)], min_val=1, max_val=ROWLEN // GROUP)
                    with pe.Fori(0, (groups + (WGROUPS - 1)) // WGROUPS) as w:
                        k = pe.snap(count, min_val=0, max_val=1 << 17)
                        pe.wait_ge(s_accread, k)
                        pe.matmul(psA[:], ones_bf[:], zeros_bf[:], start=True, stop=False)
                        pe.wait_ge(s_scaled, k + 1)
                        add_groups(groups_here(pe, groups - w * WGROUPS), k)
                        pe.matmul(psA[:], ones_bf[:], zeros_bf[:], start=False, stop=True).then_inc(s_acc, 1)
                        pe.drain().then_inc(s_free[0], 1)
                        bump(pe, count)

            norm(1, w1_sb[:])

            pe.wait_ge(s_spread_in, 1)
            pe.matmul(psM[:, 0:T], ones_row[0:1, :], groups_f[0:1, :], start=True, stop=True).then_inc(s_spread, 1)
            pe.wait_ge(s_onehot, 1)
            for h in range(2):
                cols = w_bf[:, h * BANK:(h + 1) * BANK]
                pe.matmul(psV[:, h * BANK:(h + 1) * BANK], upper_bf[:], cols, start=True, stop=True)
                last = pe.matmul(psH[h][:], ones_bf[:], cols, start=True, stop=True)
            last.then_inc(s_counted, 1)

            with pe.Fori(0, T // BATCH) as c:
                for b in range(WORDS // P):
                    pe.wait_ge(s_bits, c * (WORDS // P) + (b + 1))
                    if b == 0:
                        pe.wait_ge(s_relu, c)
                        pe.wait_ge(s_row[1], T // BATCH)
                    for k in range(PLANES):
                        at = (k * (WORDS // P) + b) * D
                        for i in range(3):
                            last = pe.matmul(psA[:], y_part[i][:, at:at + D], bit_rows[b % BPLANES][:, k, :],
                                             start=(b == 0 and k == 0 and i == 0),
                                             stop=(b == WORDS // P - 1 and k == PLANES - 1 and i == 2))
                    last.then_inc(s_bitsfree, 1)
                pe.drain().then_inc(s_sum, 1)
                pe.wait_ge(s_relu, c + 1)
                pe.wait_ge(s_prow, c)
                for j in range(BATCH):
                    last = pe.transpose(psT[1][:, j, :], outT[:, j, :], ident[:])
                last.then_inc(s_ptr, 1)

        @block.vector
        def _(dve):
            spare = register(dve, "dve_spare")
            dve.memset(eps_col[:], EPS)
            dve.memset(ones_bf[:], 1.0)
            dve.memset(zeros_bf[:], 0.0)
            dve.memset(unused[:], UNUSED)
            dve.memset(zeros_u[:], 0)
            dve.memset(more_list[:], 0)
            dve.memset(lsum[:], 0.0)
            dve.memset(acc[:], 0.0)
            for f in range(2):
                dve.sem_inc(s_free[f], 2)
            dve.sem_inc(s_prowfree, 2)
            dve.sem_inc(s_bitsfree, BPLANES)
            dve.wait_ge(s_c1, 8)
            dve.tensor_copy(ident_bf[:], ident[:])
            dve.tensor_copy(upper_bf[:], upper[:])
            dve.tensor_copy(class_no[:], class_i[:])
            for k in range(PLANES):
                dve.tensor_scalar(bit_ident[:, k, :], ident[:], float(2 ** (k + 1)), None, ALU.mult)
                dve.memset(bit_mask[:, k:k + 1], WORDS << k)
            dve.tensor_scalar(bit_node[:], iota8[:], float(WORDS), 1.0, ALU.mult, ALU.add)
            dve.tensor_scalar(chunk_base[:], iota8[:], float(WORDS), float(1 - WORDS), ALU.mult, ALU.add)
            hi, lo = bits[:].rearrange("p a b -> p (a b)"), node[:].rearrange("p a b -> p (a b)")
            for at in range(0, WORDS, LIGHT * PLANES):
                n = min(LIGHT * PLANES, WORDS - at)
                dve.drain()
                dve.tensor_scalar(hi[:, 0:n], word_i[:, at:at + n], WORDS - 8, None, ALU.bitwise_and)
                dve.drain()
                dve.tensor_scalar(V[:, at:at + n], hi[:, 0:n], 1.0 / VSCALE, None, ALU.mult)
                dve.drain()
                dve.tensor_scalar(hi[:, 0:n], word_i[:, at:at + n], 7, None, ALU.bitwise_and)
                dve.tensor_scalar(V[:, at:at + n], V[:, at:at + n], ident[:, 0:1], None, ALU.mult)
                dve.drain()
                dve.tensor_scalar(lo[:, 0:n], hi[:, 0:n], 1.0 / VSCALE, None, ALU.mult)
                dve.drain()
                dve.scalar_tensor_tensor(word_no[:, at:at + n], lo[:, 0:n], ident[:, 1:2], V[:, at:at + n],
                                         ALU.mult, ALU.add)
            dve.wait_ge(s_w, 80)
            dve.tensor_scalar(b0_rep[:], ones_row[:], b0_col[:, 0:1], None, ALU.mult)
            dve.drain().then_inc(s_const, 1)
            dve.wait_ge(s_waug, 1)
            dve.tensor_copy(w0_aug[:], psH[0][:, 0:D + 2])
            dve.tensor_copy(b0_aug[:], psH[1][:, 0:D + 2])
            dve.drain().then_inc(s_waug_sb, 1)

            def norm(layer):
                with dve.Fori(0, T) as t:
                    dve.bn_stats(stats[:, bass.ds(t, 1), :].rearrange("p a c -> p (a c)"),
                                 xs[:, bass.ds(t, 1), :].rearrange("p a c -> p (a c)"))
                dve.drain()
                for t in range(T):
                    dve.bn_aggr(mv[:, t, :], stats[:, t, :])
                dve.drain().then_inc(s_var[layer], 1)
                dve.wait_ge(s_std[layer], 1)
                dve.reciprocal(rstd[:], rstd[:])
                dve.drain()

                def normalize(b, u):
                    for j in range(BATCH):
                        t = b * BATCH + j
                        last = dve.tensor_scalar(hn[u][:, j, :], xs[:, bass.ds(t, 1), :].rearrange("p a c -> p (a c)"),
                                                 mv[:, bass.ds(t, 1), 0], rstd[:, bass.ds(t, 1)],
                                                 ALU.subtract, ALU.mult)
                    last.then_inc(s_hn[layer], 1)

                def plus(to, product, bias):
                    dve.tensor_tensor(to, product, bias, ALU.add)

                normalize(0, 0)
                with dve.Fori(0, T // BATCH // 2) as bp:
                    for u in range(2):
                        b = 2 * bp + u
                        with dve.If(b < T // BATCH - 1):
                            normalize(bounded(dve, b + 1, 1, T // BATCH - 1), 1 - u)
                        dve.wait_ge(s_mm[layer], b + 1)
                        product = psH[u][:].rearrange("p (j d) -> p j d", d=D)
                        rows = stage[u][:, :, 0:D]
                        if layer == 0:
                            dve.wait_ge(s_tab[u], bp * 16)
                            sr = psV[:, u * BANK:u * BANK + 2 * BATCH].rearrange("p (j c) -> p j c", c=2)
                            plus(rows, product, b0_aug[:, 0:D].unsqueeze(1).to_broadcast([P, BATCH, D]))
                            plus(stage[u][:, :, D], sr[:, :, 1], b0_aug[:, D + 1:D + 2].to_broadcast([P, BATCH]))
                            plus(s_col[:, bass.ds(b * BATCH, BATCH)], sr[:, :, 0],
                                 b0_aug[:, D:D + 1].to_broadcast([P, BATCH]))
                            dve.drain().then_inc(s_row[layer], 1)
                            plus(acc4[:], acc4[:], rows)
                        else:
                            hi, mid, lo = (y_part[i][:, bass.ds(b * (BATCH * D), BATCH * D)].rearrange(
                                "p (j d) -> p j d", d=D) for i in range(3))
                            dve.tensor_copy(hi, product)
                            dve.drain()
                            dve.tensor_tensor(rows, product, hi, ALU.subtract)
                            dve.drain()
                            dve.tensor_copy(mid, rows)
                            dve.drain()
                            dve.tensor_tensor(lo, rows, mid, ALU.subtract)
                            dve.drain().then_inc(s_row[layer], 1)

            dve.memset(acc4[:], 0.0)
            dve.wait_ge(s_xin, 16)
            norm(0)
            dve.drain().then_inc(s_colsum, 1)
            dve.wait_ge(s_colsum, 2)
            dve.tensor_reduce(part[0:1, :], psM[0:1, :].rearrange("p (j d) -> p d j", d=D), AX.X, ALU.add)
            dve.drain()
            dve.tensor_scalar(neutral[0:1, 0:D], part[0:1, :], 1.0 / N, None, ALU.mult)
            dve.memset(neutral[0:1, D:D + 1], MASKED)
            dve.drain().then_inc(s_neutral, 3)

            fills = register(dve, "dve_fills")
            stores = register(dve, "dve_stores")
            chunks = register(dve, "dve_chunks")

            groups_now = register(dve, "dve_groups_now")
            groups_next = register(dve, "dve_groups_next")

            deg_next = register(dve, "dve_deg_next")

            def load_degree(t):
                hold(dve, s_meta, t + 1)
                dve.reg_mov(deg_next, dve.value_load(meta_deg[0:1, bass.ds(t, 1)], min_val=1, max_val=N))

            def meta(t):
                dve.wait_ge(s_degT, t + 1)
                dve.tensor_copy(row_degree[:, bass.ds(t, 1)], degree[:])
                dve.reduce_max(mdeg[0:1, 0:1], psM[0:1, 0:P], axis=AX.X)
                dve.drain()
                dve.tensor_scalar(meta_deg[0:1, bass.ds(t, 1)], mdeg[0:1, 0:1], 1.0, None, ALU.max)
                dve.tensor_scalar(meta_groups[0:1, bass.ds(t, 1)], mdeg[0:1, 0:1],
                                  1.0, float(GROUP - 1), ALU.max, ALU.add)
                dve.drain()
                dve.tensor_scalar(meta_groups[0:1, bass.ds(t, 1)], meta_groups[0:1, bass.ds(t, 1)],
                                  2, None, ALU.logical_shift_right)
                dve.drain().then_inc(s_meta, 1)

            def wait_fill():
                n = dve.snap(fills, min_val=0, max_val=1 << 12)
                hold(dve, s_fill, n + 1)
                bump(dve, fills)

            def wait_stored():
                n = dve.snap(stores, min_val=0, max_val=1 << 12)
                dve.wait_ge(s_stored, n * 16)
                bump(dve, stores)

            def to_nodes(n):
                dve.tensor_scalar(words_i[:, 0:n], words[:, 0:n], VSCALE, None, ALU.mult)
                dve.drain()
                dve.tensor_scalar(words_no[:, 0:n], words_i[:, 0:n], WORDS - 1, None, ALU.bitwise_and)
                dve.tensor_tensor(bits[:, 0:n, :], words_i[:, 0:n].unsqueeze(2).to_broadcast([P, n, PLANES]),
                                  bit_mask[:].unsqueeze(1).to_broadcast([P, n, PLANES]), ALU.bitwise_and)
                dve.drain()
                dve.tensor_tensor(node[:, 0:n, :], words_no[:, 0:n].unsqueeze(2).to_broadcast([P, n, PLANES]),
                                  bit_node[:].unsqueeze(1).to_broadcast([P, n, PLANES]), ALU.add)
                dve.drain()
                flat = flat_nodes(n)
                dve.scalar_tensor_tensor(flat, bits[:, 0:n, :].rearrange("p a b -> p (a b)"), 0.0, flat,
                                         ALU.is_gt, ALU.mult)
                dve.drain()

            def expand(n, deg):
                to_nodes(n)
                flat = flat_nodes(n)
                dve.max(found[:, 0:8], flat)
                for r in range(8, n, 8):
                    with dve.If(deg > r):
                        dve.drain()
                        dve.match_replace(flat, found[:, r - 8:r], flat, 0.0)
                        dve.drain()
                        dve.max(found[:, r:r + 8], flat)
                dve.drain()

            def flat_nodes(n):
                return node[:, 0:n, :].rearrange("p a b -> p (a b)")

            def extract_narrow():
                dve.memset(found[:, 0:WSLOTS], 0.0)
                wait_fill()
                dve.max(words[:, 0:8], psV[:])
                dve.drain()
                dve.match_replace(V[:], words[:, 0:8], psV[:], 0.0).then_inc(s_drained, 1)
                dve.drain()
                dve.max(words[:, 8:16], V[:])
                dve.drain()
                to_nodes(NARROW)
                flat = flat_nodes(NARROW)
                dve.max(found[:, 0:8], flat)
                dve.drain()
                dve.match_replace(flat, found[:, 0:8], flat, 0.0)
                dve.drain()
                dve.max(found[:, 8:16], flat)
                dve.drain()
                wait_stored()
                dve.tensor_copy(slots_out[:, 0:LIGHT_STORE], found[:])
                dve.drain().then_inc(s_slots, 1)

            def extract_light(deg):
                dve.memset(words[:], 0.0)
                dve.memset(found[:], 0.0)
                wait_fill()
                dve.drain()
                dve.max(words[:, 0:8], psV[:])
                dve.drain()
                with dve.If(deg > 8):
                    dve.match_replace(V[:], words[:, 0:8], psV[:], 0.0).then_inc(s_drained, 1)
                    dve.drain()
                    dve.max(words[:, 8:16], V[:])
                with dve.Else():
                    dve.sem_inc(s_drained, 1)
                for r in range(16, LIGHT, 8):
                    with dve.If(deg > r):
                        dve.drain()
                        dve.match_replace(V[:], words[:, r - 8:r], V[:], 0.0)
                        dve.drain()
                        dve.max(words[:, r:r + 8], V[:])
                dve.drain()
                with dve.If(deg > MIDDLE):
                    expand(LIGHT, deg)
                    bump(dve, spare)
                with dve.Else():
                    expand(MIDDLE, deg)
                    bump(dve, spare)
                wait_stored()
                dve.tensor_copy(slots_out[:, 0:LIGHT_STORE], found[:])
                dve.drain().then_inc(s_slots, 1)

            def extract_heavy(t):
                groups = meta_groups[0:1, bass.ds(t, 1)]
                dve.memset(mdeg[0:1, 1:2], 0.0)
                wait_fill()
                dve.sem_inc(s_drained, 1)
                with dve.Fori(0, PLANES) as c:
                    wait_fill()
                    dve.drain()
                    dve.tensor_scalar(V[:], psV[:], 2.0, 0.0, ALU.is_ge, ALU.add, accum_out=cdeg[:, 0:1])
                    dve.drain().then_inc(s_cdeg, 1)
                    dve.tensor_copy(V[:], psV[:]).then_inc(s_drained, 1)
                    wait_stored()
                    dve.memset(slots_out[:], 0)
                    bump(dve, chunks)
                    n = dve.snap(chunks, min_val=0, max_val=1 << 12)
                    dve.wait_ge(s_cT, n)
                    dve.reduce_max(mdeg[0:1, 0:1], psH[1][0:1, 0:P], axis=AX.X)
                    dve.drain()
                    rounds = chunk_rounds[0:1, bass.ds(c, 1)]
                    dve.tensor_scalar(rounds, mdeg[0:1, 0:1], 7.0, None, ALU.add)
                    dve.drain()
                    dve.tensor_scalar(rounds, rounds, 3, None, ALU.logical_shift_right)
                    dve.drain()
                    dve.scalar_tensor_tensor(mdeg[0:1, 1:2], rounds, 2.0, mdeg[0:1, 1:2], ALU.mult, ALU.add)
                    dve.drain().then_inc(s_cm, 1)
                    hold(dve, s_cm, n)
                    todo = dve.value_load(rounds, min_val=0, max_val=WORDS // 8)
                    with dve.If(todo > 0):
                        with dve.Fori(0, todo) as r:
                            dve.max(top8[:], V[:])
                            dve.drain()
                            dve.match_replace(V[:], top8[:], V[:], 0.0)
                            dve.tensor_scalar(top8n[:], top8[:], VSCALE, chunk_base[:, bass.ds(c, 1)],
                                              ALU.mult, ALU.add)
                            dve.drain()
                            dve.scalar_tensor_tensor(slots_out[:, bass.ds(r * 8, 8)], top8[:], 2.0, top8n[:],
                                                     ALU.is_ge, ALU.mult)
                            dve.drain()
                        bump(dve, spare)
                    dve.drain().then_inc(s_slots, 1)
                dve.tensor_scalar(groups, mdeg[0:1, 1:2], 1.0, None, ALU.max)
                dve.drain()

            def extract(t):
                deg = dve.snap(deg_next, min_val=1, max_val=N)
                dve.reg_mov(groups_next, (deg + (GROUP - 1)) // GROUP)
                with dve.If(deg <= NARROW):
                    extract_narrow()
                with dve.Else():
                    with dve.If(deg <= LIGHT):
                        extract_light(deg)
                    with dve.Else():
                        extract_heavy(t)
                        dve.reg_mov(groups_next, dve.value_load(meta_groups[0:1, bass.ds(t, 1)], min_val=1,
                                                                max_val=ROWLEN // GROUP))
                dve.drain().then_inc(s_groups, 1)

            count = register(dve, "dve_k")

            rows_seen = gathered_counts(dve, 0)

            def add_up(k):
                dve.wait_ge(s_acc, k)
                dve.tensor_reduce(part[:], psA[:].rearrange("p (j d) -> p d j", d=D), AX.X, ALU.add).then_inc(
                    s_accread, 1)
                dve.drain()
                dve.scalar_tensor_tensor(acc[:], acc[:], alpha[:, 0:1], part[:], ALU.mult, ALU.add)
                dve.drain()

            def close_tile(t):
                dve.reciprocal(linv[:], lsum[:])
                dve.drain()
                row = xs[:, bass.ds(t, 1), :].rearrange("p a c -> p (a c)")
                dve.scalar_tensor_tensor(row, acc[:], linv[:, 0:1], row, ALU.mult, ALU.add)

            def between(t):
                k = dve.snap(count, min_val=0, max_val=1 << 17)
                dve.wait_ge(s_acc, k)
                dve.tensor_reduce(part[:], psA[:].rearrange("p (j d) -> p d j", d=D), AX.X, ALU.add).then_inc(
                    s_accread, 1)
                dve.reciprocal(linv[:], lsum[:])
                dve.drain()
                dve.scalar_tensor_tensor(acc[:], acc[:], alpha[:, 0:1], part[:], ALU.mult, ALU.add)
                dve.drain()
                at = t - 1 if isinstance(t, int) else bounded(dve, t - 1, 0, T - 4)
                row = xs[:, bass.ds(at, 1), :].rearrange("p a c -> p (a c)")
                dve.scalar_tensor_tensor(row, acc[:], linv[:, 0:1], row, ALU.mult, ALU.add)
                dve.memset(m_old[:], LOWEST)

            def weigh(k, first, n):
                rows = gathered[:, bass.ds((k % 2) * WSLOTS + first, n), 0:D]
                dve.tensor_tensor(rows, rows, prob[:, first:first + n].unsqueeze(2).to_broadcast([P, n, D]), ALU.mult)

            def attend_window(t, k, rest):
                n = groups_here(dve, rest)
                r_col = gathered[:, bass.ds((k % 2) * WSLOTS, WSLOTS), D]
                wait_gathered(dve, 0, rows_seen, k + 1, n)
                dve.tensor_scalar(e_raw[:], r_col, s_col[:, bass.ds(t, 1)], None, ALU.add)
                dve.drain()
                dve.scalar_tensor_tensor(e_sc[:], e_raw[:], ALPHA, e_raw[:], ALU.mult, ALU.max)
                dve.tensor_copy(r_col, unused[:])
                dve.drain()
                dve.reduce_max(m_win[:], e_sc[:], axis=AX.X)
                dve.drain()
                dve.tensor_scalar(m_neg[:], m_win[:], m_old[:, 0:1], -1.0, ALU.max, ALU.mult)
                dve.drain().then_inc(s_e, 1)
                dve.wait_ge(s_p, k + 1)
                weigh(k, 0, 2 * GROUP)
                with dve.If(n > 2):
                    weigh(k, 2 * GROUP, 2 * GROUP)
                with dve.If(n > 4):
                    weigh(k, 4 * GROUP, 2 * GROUP)
                with dve.If(n > 6):
                    weigh(k, 6 * GROUP, 2 * GROUP)
                dve.tensor_scalar(m_old[:], m_neg[:], -1.0, None, ALU.mult)
                dve.scalar_tensor_tensor(lsum[:], lsum[:], alpha[:, 0:1], lwin[:], ALU.mult, ALU.add)
                dve.drain().then_inc(s_scaled, 1)

            meta(0)
            load_degree(0)
            extract(0)
            meta(1)
            load_degree(1)

            def attend(t):
                groups = dve.snap(groups_now, min_val=1, max_val=ROWLEN // GROUP)
                with dve.Fori(0, (groups + (WGROUPS - 1)) // WGROUPS) as w:
                    k = dve.snap(count, min_val=0, max_val=1 << 17)
                    with dve.If(w > 0):
                        add_up(k)
                        bump(dve, spare)
                    attend_window(t, k, groups - w * WGROUPS)
                    bump(dve, count)

            def advance():
                dve.reg_mov(groups_now, dve.snap(groups_next, min_val=1, max_val=ROWLEN // GROUP))

            def prepare(t):
                meta(t)
                load_degree(t)

            advance()
            extract(1)
            dve.memset(m_old[:], LOWEST)
            attend(0)
            prepare(2)
            with dve.Fori(1, T - 2) as t:
                advance()
                extract(bounded(dve, t + 1, 2, T - 2))
                between(t)
                attend(t)
                prepare(bounded(dve, t + 2, 3, T - 1))
            for t in (T - 2, T - 1):
                advance()
                if t < T - 1:
                    extract(t + 1)
                between(t)
                attend(t)
            add_up(dve.snap(count, min_val=0, max_val=1 << 17))
            close_tile(T - 1)
            dve.drain()

            norm(1)

            def rank_rows():
                dve.tensor_copy(groups_f[:], meta_groups[:])
                dve.tensor_scalar(ranked[:, :, 0], row_no[:], ROWWINDOWS.bit_length() - 1, None,
                                  ALU.logical_shift_left)
                dve.tensor_scalar(row_groups[:], row_degree[:], 1.0, float(GROUP - 1), ALU.max, ALU.add)
                dve.drain().then_inc(s_spread_in, 1)
                dve.tensor_scalar(row_groups[:], row_groups[:], 2, None, ALU.logical_shift_right)
                dve.wait_ge(s_spread, 1)
                dve.tensor_copy(tile_groups[:], psM[:, 0:T])
                dve.drain()
                dve.scalar_tensor_tensor(tile_groups[:], tile_groups[:], float(LIGHT // GROUP), tile_groups[:],
                                         ALU.is_gt, ALU.mult)
                dve.drain()
                dve.tensor_tensor(tile_groups[:], tile_groups[:], row_groups[:], ALU.max)
                dve.drain()
                dve.tensor_copy(ranked[:, :, 1], tile_groups[:])
                dve.tensor_scalar(row_class[:], tile_groups[:], float(CLASSES - 1), None, ALU.min)
                dve.drain()
                dve.tensor_tensor(one_hot, row_class[:].unsqueeze(1).to_broadcast([P, CLASSES, T]),
                                  class_no[:].unsqueeze(2).to_broadcast([P, CLASSES, T]), ALU.is_equal)
                dve.drain().then_inc(s_onehot, 1)
                dve.wait_ge(s_counted, 1)
                for h in range(2):
                    dve.tensor_copy(V[:, h * BANK:(h + 1) * BANK], psH[h][:])
                step, a = 1, V[:]
                b = slots_out[:].bitcast(F32)
                while step < WORDS:
                    dve.drain()
                    dve.tensor_copy(b[:, 0:step], a[:, 0:step])
                    dve.tensor_tensor(b[:, step:WORDS], a[:, step:WORDS], a[:, 0:WORDS - step], ALU.add)
                    a, b = b, a
                    step *= 2
                dve.drain()
                for h in range(2):
                    half = a[:, h * BANK:(h + 1) * BANK]
                    dve.tensor_tensor(half, half, psH[h][:], ALU.subtract)
                dve.drain()
                dve.tensor_tensor(a, a, psV[:], ALU.add)
                dve.drain()
                dve.tensor_tensor(a, a, w_bf[:], ALU.mult)
                dve.drain()
                dve.tensor_reduce(rank_f[:], a.rearrange("p (c t) -> p t c", t=T), AX.X, ALU.add)
                dve.drain()
                dve.tensor_copy(rank[:], rank_f[:])
                dve.drain().then_inc(s_ranked, 1)

            rank_rows()

            with dve.Fori(0, T // BATCH // 2) as cp:
                for u in range(2):
                    c = 2 * cp + u
                    dve.wait_ge(s_wordsin[u], (cp + 1) * 16)
                    for b in range(WORDS // P):
                        dve.wait_ge(s_bitsfree, c * (WORDS // P) + (b + 1))
                        for k in range(PLANES):
                            last = dve.tensor_scalar(
                                bit_rows[b % BPLANES][:, k, :].bitcast(U16).rearrange("p (u n) -> p u n", n=P),
                                words_in[u][:, :, b * P:(b + 1) * P], 14 - k, 1 << 14,
                                ALU.logical_shift_left, ALU.bitwise_and)
                        last.then_inc(s_bits, 1)
                    dve.drain().then_inc(s_unpacked, 1)
            dve.memset(neutral[0:1, :], LOWEST)
            dve.drain().then_inc(s_neutral, 1)
            dve.wait_ge(s_sorted_t, 16)
            dve.tensor_reduce(sorted_max[:], sorted_t[:, :, 1], AX.X, ALU.max)
            dve.drain().then_inc(s_max, 1)
            dve.wait_ge(s_sorted, 16)
            hold(dve, s_maxin, 16)
            rows_max = gathered_counts(dve, 1)

            def start_max(t):
                dve.memset(acc4[:], LOWEST)
                dve.tensor_copy(window_no[:], sorted_rows[:, bass.ds(t, 1), 0])
                dve.tensor_copy(groups_left[:], sorted_rows[:, bass.ds(t, 1), 1])
                dve.drain()

            def next_lists():
                dve.tensor_scalar(window_no[:], window_no[:], 1.0, None, ALU.add)
                dve.tensor_scalar(groups_left[:], groups_left[:], float(-WGROUPS), None, ALU.add)
                dve.drain()
                dve.tensor_scalar(past_end[:], groups_left[:], 0.0, float(N * ROWWINDOWS), ALU.is_le, ALU.mult)
                dve.drain()
                dve.tensor_tensor(more_index[:], past_end[:], window_no[:], ALU.add)
                dve.drain().then_inc(s_index, 1)

            def add_max(t, w, k, rest, groups):
                with dve.If(rest > WGROUPS):
                    next_lists()
                    bump(dve, spare)
                n = groups_here(dve, rest)
                wait_gathered(dve, 1, rows_max, k + 1, n)
                with dve.Fori(0, n) as g:
                    dve.tensor_tensor(acc4[:], acc4[:], gathered[:, bass.ds(slot_at(k, g), GROUP), 0:D], ALU.max)
                    dve.drain()
                dve.drain().then_inc(s_free[1], 1)

            def end_max(t):
                dve.tensor_reduce(part[:], acc4[:].rearrange("p j d -> p d j"), AX.X, ALU.max)
                dve.drain()
                for b in range(2):
                    with (dve.If(t % 2 == 0) if b == 0 else dve.Else()):
                        hold(dve, s_added[b], (t // 2) * 16)
                dve.tensor_copy(stage2[:, bass.ds(t % 2, 1), :].rearrange("p a d -> p (a d)"), part[:])
                dve.tensor_scalar(out_row[:, bass.ds(t % 2, 1)], sorted_rows[:, bass.ds(t, 1), 0],
                                  ROWWINDOWS.bit_length() - 1, None, ALU.logical_shift_right)
                dve.drain().then_inc(s_orow, 1)

            windows(dve, "dve2", add_max, start_max, end_max, counts=sorted_groups)


_INS = ["x", "adj", "L0_gnn_W", "L0_gnn_b", "L0_gnn_a_s", "L0_gnn_a_r", "L1_gnn_weight", "L1_gnn_bias"]


def kernel(**inputs):
    import numpy as np
    import concourse.bacc as bacc
    from concourse.bass_utils import run_bass_kernel_spmd

    nc = bacc.Bacc("TRN2", target_bir_lowering=False, num_devices=1)
    arrays, args = {}, []
    for name in _INS:
        a = np.ascontiguousarray(inputs[name])
        arrays[f"in_{name}"] = a
        args.append(nc.dram_tensor(f"in_{name}", a.shape, mybir.dt.from_np(a.dtype), kind="ExternalInput").ap())
    out = nc.dram_tensor("out_0", (N, D), F32, kind="ExternalOutput").ap()
    build(nc, *args, out)
    r = run_bass_kernel_spmd(nc, [arrays], core_ids=[0])
    return r.results[0]["out_0"]
```
